# Optimizing a Trainium2 kernel written in Bass

```python
import numpy as np
import jax
import jax.numpy as jnp

def _softmax(x, axis=-1):
    return jax.nn.softmax(x, axis=axis)

def _gelu(x):
    return jax.nn.gelu(x, approximate=True)

def _silu(x):
    return jax.nn.silu(x)

def _sigmoid(x):
    return jax.nn.sigmoid(x)

def _layernorm(x, axis=-1, eps=1e-05):
    m = jnp.mean(x, axis=axis, keepdims=True)
    v = jnp.var(x, axis=axis, keepdims=True)
    return (x - m) / jnp.sqrt(v + eps)

def _scatter_add(tgt, idx, src, axis=0):
    return tgt.at[idx].add(src)

def _segment_sum(src, seg, n):
    return jax.ops.segment_sum(src, seg, n)
kernel_name = 'mk_xattn_ffn_d1_seqx_r8_af6698'

def setup_inputs(seed: int=0):
    np.random.seed(seed)
    _w = jnp.asarray

    def _rec_inputs():
        import jax
        import jax.numpy as jnp
        _rk = jax.random.key(seed)
        x = 7.22e-05 + 1 * jax.random.normal(jax.random.fold_in(_rk, 1), (8, 128, 512), jnp.float32)
        _lenS = 128 - jax.random.randint(jax.random.fold_in(_rk, 7), (8,), 0, max(1, 128 // 4) + 1, jnp.int32)
        _lenS2 = 128 - jax.random.randint(jax.random.fold_in(_rk, 8), (8,), 0, max(1, 128 // 4) + 1, jnp.int32)
        _ctx_4096P = jax.random.normal(jax.random.fold_in(_rk, 11), (8, 16, 512), jnp.float32)
        _ctx_4096c = jax.random.dirichlet(jax.random.fold_in(_rk, 511), 0.3 * jnp.ones((16,), jnp.float32), (8, 128))
        _ctx_4096t = jnp.einsum('bsk,bkd->bsd', _ctx_4096c, _ctx_4096P)
        _ctx_4096t = _ctx_4096t * jax.lax.rsqrt(jnp.mean(jnp.square(_ctx_4096t)) + 1e-12) * 0.953939
        ctx_4096 = 4.13588e-05 + 0.999923 * (_ctx_4096t + 0.3 * jax.random.normal(jax.random.fold_in(_rk, 611), (8, 128, 512), jnp.float32))
        _validS = jnp.arange(128)[None, :] < _lenS[:, None]
        _validS2 = jnp.arange(128)[None, :] < _lenS2[:, None]
        _causal = jnp.tril(jnp.ones((128, 128), dtype=bool))
        mask_BxSxS2_bk0 = jnp.logical_not(jnp.broadcast_to(_validS2[:, None, :], (8, 128, 128)))
        return (x, ctx_4096, mask_BxSxS2_bk0)
    x, ctx_4096, mask_BxSxS2_bk0 = _rec_inputs()

    def _L0_xattn_setup():
        import jax, jax.numpy as jnp
        import numpy as np
        B, LQ, LK, D, H, DH = (2, 128, 128, 512, 32, 128)
        EPS = 1e-05

        def _rmsnorm(x, weight):
            var = jnp.mean(jnp.square(x), axis=-1, keepdims=True)
            return x * jax.lax.rsqrt(var + EPS) * weight
        key = jax.random.key(seed)
        ks = jax.random.split(key, 8)
        scale = 0.02
        return {'hidden_states': jax.random.normal(ks[0], (B, LQ, D), jnp.float32), 'key_value_states': jax.random.normal(ks[1], (B, LK, D), jnp.float32), 'attention_mask': jax.random.randint(ks[2], (B, LQ, LK), 0, 2) > 0, 'position_bias': jax.random.normal(ks[3], (H, LQ, LK), jnp.float32), 'ln_weight': jnp.ones((D,), jnp.float32), 'w_q': jax.random.normal(ks[4], (H * DH, D), jnp.float32) * scale, 'w_k': jax.random.normal(ks[5], (H * DH, D), jnp.float32) * scale, 'w_v': jax.random.normal(ks[6], (H * DH, D), jnp.float32) * scale, 'w_out': jax.random.normal(ks[7], (D, H * DH), jnp.float32) * scale}
    _L0_xattn_all = _L0_xattn_setup()
    _L0_xattn_in = {k: v for k, v in _L0_xattn_all.items() if k in ('position_bias', 'ln_weight', 'w_q', 'w_k', 'w_v', 'w_out')}
    del _L0_xattn_all

    def _L0_ffn_setup():
        import jax, jax.numpy as jnp
        import numpy as np
        HIDDEN = 512
        INTER = 1376
        SPARSITY = 0.5

        def _ternary_weight(key, out_dim, in_dim, sparsity):
            k_mask, k_sign = jax.random.split(key)
            nonzero = jax.random.bernoulli(k_mask, 1.0 - sparsity, (out_dim, in_dim))
            sign = jnp.where(jax.random.bernoulli(k_sign, 0.5, (out_dim, in_dim)), 1.0, -1.0)
            return (nonzero * sign).astype(jnp.float32)
        key = jax.random.key(seed)
        kx, kg, ku, kd, ksg, ksu, ksd = jax.random.split(key, 7)
        x = jax.random.normal(kx, (4, 256, HIDDEN), dtype=jnp.float32)
        Wg = _ternary_weight(kg, INTER, HIDDEN, SPARSITY)
        Wu = _ternary_weight(ku, INTER, HIDDEN, SPARSITY)
        Wd = _ternary_weight(kd, HIDDEN, INTER, SPARSITY)
        ag = jax.random.uniform(ksg, (INTER,), dtype=jnp.float32, minval=0.5, maxval=1.5) / np.sqrt(HIDDEN)
        au = jax.random.uniform(ksu, (INTER,), dtype=jnp.float32, minval=0.5, maxval=1.5) / np.sqrt(HIDDEN)
        ad = jax.random.uniform(ksd, (HIDDEN,), dtype=jnp.float32, minval=0.5, maxval=1.5) / np.sqrt(INTER)
        return {'x': x, 'Wg': Wg, 'Wu': Wu, 'Wd': Wd, 'ag': ag, 'au': au, 'ad': ad}
    _L0_ffn_all = _L0_ffn_setup()
    _L0_ffn_in = {k: v for k, v in _L0_ffn_all.items() if k in ('Wg', 'Wu', 'Wd', 'ag', 'au', 'ad')}
    del _L0_ffn_all
    return {'x': x, 'ctx_4096': ctx_4096, 'mask_BxSxS2_bk0': mask_BxSxS2_bk0, 'L0_xattn_position_bias': _L0_xattn_in['position_bias'], 'L0_xattn_ln_weight': _L0_xattn_in['ln_weight'], 'L0_xattn_w_q': _L0_xattn_in['w_q'], 'L0_xattn_w_k': _L0_xattn_in['w_k'], 'L0_xattn_w_v': _L0_xattn_in['w_v'], 'L0_xattn_w_out': _L0_xattn_in['w_out'], 'L0_ffn_Wg': _L0_ffn_in['Wg'], 'L0_ffn_Wu': _L0_ffn_in['Wu'], 'L0_ffn_Wd': _L0_ffn_in['Wd'], 'L0_ffn_ag': _L0_ffn_in['ag'], 'L0_ffn_au': _L0_ffn_in['au'], 'L0_ffn_ad': _L0_ffn_in['ad']}

def reference(x, ctx_4096, mask_BxSxS2_bk0, L0_xattn_position_bias, L0_xattn_ln_weight, L0_xattn_w_q, L0_xattn_w_k, L0_xattn_w_v, L0_xattn_w_out, L0_ffn_Wg, L0_ffn_Wu, L0_ffn_Wd, L0_ffn_ag, L0_ffn_au, L0_ffn_ad):
    import jax
    import jax.numpy as jnp

    def _L0_xattn_ref(hidden_states, key_value_states, attention_mask, position_bias, ln_weight, w_q, w_k, w_v, w_out):
        import jax, jax.numpy as jnp
        import numpy as np
        B, LQ, LK, D, H, DH = (2, 128, 128, 512, 32, 128)
        EPS = 1e-05

        def _rmsnorm(x, weight):
            var = jnp.mean(jnp.square(x), axis=-1, keepdims=True)
            return x * jax.lax.rsqrt(var + EPS) * weight
        x = _rmsnorm(hidden_states, ln_weight)
        b, lq, _ = x.shape
        lk = key_value_states.shape[1]
        h_q = (x @ w_q.T).reshape(b, lq, H, DH)
        h_k = (key_value_states @ w_k.T).reshape(b, lk, H, DH)
        h_v = (key_value_states @ w_v.T).reshape(b, lk, H, DH)
        score = jnp.einsum('bqhd,bkhd->bhqk', h_q, h_k)
        score = score + position_bias[None]
        m = attention_mask[:, None]
        score = jnp.where(m, score, -jnp.inf)
        score = jax.nn.softmax(score, axis=-1)
        score = jnp.where(m, score, 0.0)
        attn = jnp.einsum('bhqk,bkhd->bqhd', score, h_v).reshape(b, lq, H * DH)
        out = attn @ w_out.T
        return hidden_states + out

    def _L0_ffn_ref(x, Wg, Wu, Wd, ag, au, ad):
        import jax, jax.numpy as jnp
        import numpy as np
        HIDDEN = 512
        INTER = 1376
        SPARSITY = 0.5

        def _ternary_weight(key, out_dim, in_dim, sparsity):
            k_mask, k_sign = jax.random.split(key)
            nonzero = jax.random.bernoulli(k_mask, 1.0 - sparsity, (out_dim, in_dim))
            sign = jnp.where(jax.random.bernoulli(k_sign, 0.5, (out_dim, in_dim)), 1.0, -1.0)
            return (nonzero * sign).astype(jnp.float32)
        gate = jnp.einsum('bsh,ih->bsi', x, Wg) * ag
        up = jnp.einsum('bsh,ih->bsi', x, Wu) * au
        h = jax.nn.silu(gate) * up
        out = jnp.einsum('bsi,hi->bsh', h, Wd) * ad
        return out
    x = x + _L0_xattn_ref(_layernorm(x, axis=-1), ctx_4096, mask_BxSxS2_bk0, L0_xattn_position_bias, L0_xattn_ln_weight, L0_xattn_w_q, L0_xattn_w_k, L0_xattn_w_v, L0_xattn_w_out)
    x = x + _L0_ffn_ref(_layernorm(x, axis=-1), L0_ffn_Wg, L0_ffn_Wu, L0_ffn_Wd, L0_ffn_ag, L0_ffn_au, L0_ffn_ad)
    return x

_drawn_inputs = setup_inputs


def setup_inputs(seed=0):
    import zlib

    import numpy as np

    out = dict(_drawn_inputs(seed))
    spreads = {'L0_xattn_ln_weight': (1.0, 0.2)}
    factors = {}
    for name, (base, spread) in spreads.items():
        noise = np.random.default_rng([zlib.crc32(name.encode()), seed]).standard_normal(out[name].shape)
        drawn = base * np.exp(spread * noise) if base else spread * noise
        out[name] = jnp.asarray(drawn.astype(out[name].dtype))
    for name, factor in factors.items():
        out[name] = (out[name] * factor).astype(out[name].dtype)
    return out
```

```python
import concourse.bass as bass
from concourse import mybir
from contextlib import ExitStack

B, S, D, H, DH = 8, 128, 512, 32, 128
P = 128
T = B * S
DC = D // P
GH = 2
NG = H // GH
HALF = T // 2
HB = B // 2
FF = 1376
FC = -(-FF // P)
EPS = 1e-5
MASKED = -1e30

PRO = [("k", 0), ("k", 1), ("v", 0), ("v", 1), ("q", 0), ("q", 1), ("A", 0), ("V", 0), ("A", 1)]
RING = [("A", 2), ("V", 2), ("A", 3), ("A", 4), ("A", 5), ("V", 5), ("A", 6), ("V", 6), ("A", 7),
        ("A", 8), ("V", 8), ("A", 9)]
NB = 3
V_PAIR = {2: 3, 5: 0, 6: 1, 8: 2}
O_OF = {2: [], 3: [0], 4: [1, 2], 5: [3], 6: [4], 7: [5], 8: [6], 9: [7]}
SPLIT_PRO = [("k", 0), ("k", 1), ("v", 0), ("q", 0), ("q", 1)]
SPLITS = [("o", 0), ("q", 0), ("v", 0), ("k", 0), ("q", 1), ("k", 1)]
SPLIT_OF = {2: [0, 1], 3: [2, 3], 4: [4], 5: [5]}


def ring_step(g, key):
    return g * len(RING) + (len(PRO) + RING.index(key))


def ring_bank(key):
    return RING.index(key) % NB


def a_kind(s):
    return "qkqk"[s % 4], (s % 4) // 2, 1 if s % 8 < 4 else 0


def split_count(g, n):
    return g * len(SPLITS) + (len(SPLIT_PRO) + n + 1)


def program(nc, x, ctxt, mask, bias, lnw, wq, wk, wv, wo, wg, wu, wd, ag, au, ad, out):
    f32 = mybir.dt.float32
    f32r = mybir.dt.float32r
    u8 = mybir.dt.uint8
    ALU = mybir.AluOpType
    ACT = mybir.ActivationFunctionType
    AX = mybir.AxisListType

    ctx = ExitStack()
    with ctx:
        def sb(name, shape, dt=f32):
            return ctx.enter_context(nc.sbuf_tensor(name, shape, dt))

        def sem(name):
            return ctx.enter_context(nc.semaphore(name))

        xT = [sb("xT_hi", [P, DC, T], f32r), sb("xT_lo", [P, DC, T], f32r)]
        cT = [sb("cT_hi", [P, DC, T], f32r), sb("cT_lo", [P, DC, T], f32r)]
        y = sb("y", [P, B, D])
        q = sb("q", [P, GH, T])
        k = sb("k", [P, GH, T])
        v = sb("v", [P, B, GH * DH])
        hid = [sb("hid_hi", [P, 2, T], f32r), sb("hid_lo", [P, 2, T], f32r)]
        at = [sb("at_hi", [P, HB, GH * S], f32r), sb("at_lo", [P, HB, GH * S], f32r)]
        raw = {n: sb(f"w{n}_raw", [P, GH, D]) for n in "qkvo"}
        w = {n: [sb(f"w{n}_hi", [P, GH, D], f32r), sb(f"w{n}_lo", [P, GH, D], f32r)] for n in "qkvo"}
        bias_sb = sb("bias_sb", [P, GH, S])
        maskadd = sb("maskadd", [P, B, S])
        ad_sb = maskadd[:, 0:D // S, :].rearrange("p b n -> p (b n)")
        some = sb("some", [P, B])
        bm = sb("bm", [P, 4, GH, S])
        sc = sb("sc", [P, GH, S])
        pr = sb("pr", [P, GH, S])
        pt = sb("pt", [P, GH, S])
        negmax = sb("negmax", [P, GH])
        rowsum = sb("rowsum", [P, GH])
        rinv = sb("rinv", [P, GH])
        ident = sb("ident", [P, P])
        nrm = sb("nrm", [P, HB, D])
        cstage = [raw["o"][:, :, :], bm[:, :, :, :].rearrange("p r h n -> p (r h) n")\
                  .rearrange("p (a r) n -> p a (r n)", a=2)]
        stats = sb("stats", [P, B, 6])
        mv = sb("mv", [P, B, 2])
        small = sb("small", [P, 8, B])
        minus_half = sb("minus_half", [P, B])
        lnw_sb = sb("lnw_sb", [P, DC])
        ag_sb = sb("ag_sb", [P, FC])
        au_sb = sb("au_sb", [P, FC])
        ag_now = sb("ag_now", [P, 2])
        mask_u8 = sb("mask_u8", [P, B, S], u8)
        warm = sb("warm", [P, 1])

        bank = [ctx.enter_context(nc.psum_tensor(f"bank{i}", [P, 512], f32)) for i in range(8)]
        S_BANK, T_BANK, PV_BANK, O_BANK = bank[3], bank[4], bank[5], bank[6:8]
        TURN = [0, 1]
        O_FREE, DOWN_FREE = 2, 4
        GATE, UP, DOWN = [bank[2], bank[0]], [bank[3], bank[1]], bank[4:8]

        x_in = [sem(f"x_in{i}") for i in range(2)]
        c_in = [sem(f"c_in{i}") for i in range(2)]
        consts_in = sem("consts_in")
        mask_in = sem("mask_in")
        w_in = {n: sem(f"w{n}_in") for n in "qkvo"}
        ffn_in = {n: [sem(f"ffn_w{n}_in{i}") for i in range(2)] for n in "qko"}
        bias_in = sem("bias_in")
        pool_init = sem("pool_init")
        mask_set = sem("mask_set")
        mask_ready = sem("mask_ready")
        stats_set = sem("stats_set")
        residual_set = sem("residual_set")
        stats_ready = sem("stats_ready")
        scale_step = sem("scale_step")
        scale_ready = sem("scale_ready")
        nrm_ready = sem("nrm_ready")
        turned = sem("turned")
        turned_hi = sem("turned_hi")
        turned_lo = sem("turned_lo")
        c_hi = sem("c_hi")
        c_lo = sem("c_lo")
        w_hi = sem("w_hi")
        w_lo = sem("w_lo")
        proj_done = sem("proj_done")
        proj_ready = sem("proj_ready")
        bm_ready = sem("bm_ready")
        scores_done = sem("scores_done")
        masked_ready = sem("masked_ready")
        max_ready = sem("max_ready")
        exp_done = sem("exp_done")
        rinv_ready = sem("rinv_ready")
        prob_ready = sem("prob_ready")
        pt_done = sem("pt_done")
        pt_ready = sem("pt_ready")
        pv_done = sem("pv_done")
        at_hi = sem("at_hi")
        at_lo = sem("at_lo")
        o_done = sem("o_done")
        y_added = sem("y_added")
        wd_scaled = sem("wd_scaled")
        ag_set = sem("ag_set")
        gate_done = sem("gate_done")
        up_done = sem("up_done")
        silu_done = sem("silu_done")
        h_ready = sem("h_ready")
        h_hi = sem("h_hi")
        h_lo = sem("h_lo")
        down_done = sem("down_done")
        y2_added = sem("y2_added")
        out_sent = sem("out_sent")

        block = ctx.enter_context(nc.Block())

        ATT_SPLITS = split_count(NG - 1, 0)

        def ffn_split(c, what):
            if what == "down":
                return c * 3 + (ATT_SPLITS + 5)
            return c * 3 + (ATT_SPLITS + (1 if what == "gate" else 2))

        def ffn_loaded(c, parity):
            return c * 8 + (16 - 8 * parity)

        @block.sync
        def _(sp):
            def load(n, source, g):
                src = source[bass.ds(g, 1), :, :].rearrange("o p n -> p (o n)")
                sp.dma_start(raw[n][:, :, :].rearrange("p h n -> p (h n)"), src).then_inc(w_in[n], 16)

            def load_bias(g):
                sp.dma_start(bias_sb[:, :, :].rearrange("p h n -> p (h n)"),
                             bias[bass.ds(g, 1), :, :].rearrange("o p n -> p (o n)")).then_inc(bias_in, 16)

            def load_c(half):
                for j in range(2):
                    sp.dma_start(cstage[j],
                                 ctxt[:, 2 * j:2 * j + 2, half * HALF:(half + 1) * HALF])\
                        .then_inc(c_in[j], 16)

            def load_x(half):
                for b in range(half * HB, (half + 1) * HB):
                    sp.dma_start(y[:, b, :], x[b, :, :]).then_inc(x_in[half], 16)

            load_c(0)
            load("k", wk, 0)
            load_x(0)
            load("v", wv, 0)
            sp.dma_start(lnw_sb[:, :], lnw).then_inc(consts_in, 16)
            load("q", wq, 0)
            load_x(1)
            sp.wait_ge(c_lo, 2)
            load_c(1)
            sp.dma_start(mask_u8[:, :, :], mask).then_inc(mask_in, 16)
            load_bias(0)
            sp.wait_ge(c_lo, 4)
            load("o", wo, 0)
            sp.dma_start(ag_sb[:, :], ag).then_inc(consts_in, 16)
            sp.dma_start(au_sb[:, :], au).then_inc(consts_in, 16)
            sp.wait_ge(w_lo, 3)
            load("k", wk, 1)
            load("v", wv, 1)
            sp.wait_ge(w_lo, len(SPLIT_PRO))
            load("q", wq, 1)

            def attention_loads(g, more):
                sp.wait_ge(w_lo, split_count(g, 0))
                load("o", wo, g + 1)
                if more:
                    sp.wait_ge(w_lo, split_count(g, 2))
                    load("v", wv, g + 2)
                    sp.wait_ge(w_lo, split_count(g, 4))
                    load("q", wq, g + 2)
                    sp.wait_ge(w_lo, split_count(g, 5))
                    load("k", wk, g + 2)
                sp.wait_ge(bm_ready, g * B + B)
                load_bias(g + 1)

            with sp.Fori(0, NG - 2, 1) as g:
                attention_loads(g, True)
            attention_loads(NG - 2, False)

            def load_ffn(n, source, c, parity):
                src = source[bass.ds(c, 1), :, :].rearrange("o p n -> p (o n)")
                sp.dma_start(raw[n][:, parity, :], src).then_inc(ffn_in[n][parity], 16)

            for c in range(2):
                if c == 0:
                    sp.wait_ge(w_lo, split_count(NG - 2, 5))
                load_ffn("q", wg, c, c)
                load_ffn("k", wu, c, c)
            sp.wait_ge(w_lo, ATT_SPLITS)
            sp.wait_ge(bm_ready, NG * B)
            sp.dma_start(ad_sb, ad.rearrange("(o n) -> o n", o=1).broadcast_to([P, D])).then_inc(consts_in, 16)
            load_ffn("o", wd, 0, 0)
            load_ffn("o", wd, 1, 1)

            def ffn_loads(c, parity):
                sp.wait_ge(w_lo, ffn_split(c + 1, "up"))
                load_ffn("q", wg, c + 3, 1 - parity)
                load_ffn("k", wu, c + 3, 1 - parity)
                sp.wait_ge(w_lo, ffn_split(c, "down"))
                load_ffn("o", wd, c + 2, parity)

            sp.wait_ge(w_lo, ffn_split(0, "up"))
            load_ffn("q", wg, 2, 0)
            load_ffn("k", wu, 2, 0)
            with sp.Fori(0, (FC - 3) // 2, 1) as j:
                ffn_loads(j * 2, 0)
                ffn_loads(j * 2 + 1, 1)
            sp.wait_ge(w_lo, ffn_split(FC - 3, "down"))
            load_ffn("o", wd, FC - 1, 0)
            for b in range(B):
                sp.wait_ge(y2_added, (FC - 1) * B + b + 1 + DOWN_FREE)
                sp.dma_start(out[b, :, :], y[:, b, :]).then_inc(out_sent, 16)
            sp.wait_ge(out_sent, 16 * B)

        @block.gpsimd
        def _(pool):
            pool.memset(ident[:, :], 0.0).then_inc(pool_init, 1)
            pool.memset(minus_half[:, :], -0.5).then_inc(pool_init, 1)
            pool.wait_ge(pool_init, 1)
            pool.affine_select(out=ident[:, :], in_=ident[:, :], compare_op=ALU.not_equal, fill=1.0,
                               base=0, pattern=[[-1, P]], channel_multiplier=1).then_inc(pool_init, 1)
            pool.wait_ge(pool_init, 3)
            steps = [0]

            def link(ins):
                steps[0] += 1
                ins.then_inc(scale_step, 1)
                pool.wait_ge(scale_step, steps[0])

            def scales(n, half, rms):
                h = slice(half * HB, (half + 1) * HB)
                mean, var = mv[:, h, 0], mv[:, h, 1]
                pool.wait_ge(stats_ready, n + 1)
                link(pool.tensor_scalar(small[:, 3, h], var, EPS, 1.0, ALU.add, ALU.mult))
                if not rms:
                    pool.tensor_tensor(small[:, 0, h], small[:, 3, h], minus_half[:, h], ALU.pow)\
                        .then_inc(scale_ready, 1)
                    return
                link(pool.tensor_tensor(small[:, 4, h], small[:, 3, h], minus_half[:, h], ALU.pow))
                link(pool.tensor_tensor(small[:, 5, h], var, small[:, 4, h], ALU.mult))
                link(pool.tensor_tensor(small[:, 5, h], small[:, 5, h], small[:, 4, h], ALU.mult))
                link(pool.tensor_scalar(small[:, 5, h], small[:, 5, h], EPS, 1.0, ALU.add, ALU.mult))
                link(pool.tensor_tensor(small[:, 6, h], small[:, 5, h], minus_half[:, h], ALU.pow))
                link(pool.tensor_tensor(small[:, 0, h], small[:, 6, h], small[:, 4, h], ALU.mult))
                link(pool.tensor_scalar(small[:, 1, h], small[:, 4, h], 1.0, 1.0, ALU.add, ALU.mult))
                link(pool.tensor_tensor(small[:, 7, h], mean, small[:, 4, h], ALU.mult))
                pool.tensor_scalar(small[:, 2, h], small[:, 7, h], -1.0, 0.0, ALU.mult, ALU.add)\
                    .then_inc(scale_ready, 1)

            def split_lo(count, hi, lo, source):
                pool.wait_ge(w_hi, count)
                pool.tensor_tensor(lo, source, hi, ALU.subtract).then_inc(w_lo, 1)

            def split_att(count, key):
                n, h = key
                part = (slice(None), h) if n in "qk" else (slice(None), slice(None))
                split_lo(count, w[n][0][part], w[n][1][part], raw[n][part])

            def add_bias(n, b):
                pool.tensor_tensor(bm[:, b % 4, :, :], bias_sb[:, :, :],
                                   maskadd[:, b:b + 1, :].broadcast_to([P, GH, S]), ALU.add).then_inc(bm_ready, 1)

            for n in range(2):
                split_att(n + 1, SPLIT_PRO[n])
            scales(0, 0, True)
            for n in range(2, 5):
                split_att(n + 1, SPLIT_PRO[n])
            scales(1, 1, True)
            pool.wait_ge(mask_ready, 1)
            pool.wait_ge(bias_in, 16)
            pool.wait_ge(c_lo, 4)
            for b in range(4):
                add_bias(b, b)

            def slot(g, s, last):
                for n in SPLIT_OF.get(s, []):
                    if not last or n == 0:
                        split_att(split_count(g, n), SPLITS[n])
                if s + 2 < B or not last:
                    if s == 6:
                        pool.wait_ge(bias_in, g * 16 + 32)
                    pool.wait_ge(masked_ready, g * B + (s - 2 + 1))
                    add_bias(g * B + s + 2, (s + 2) % B)

            with pool.Fori(0, NG - 1, 1) as g:
                for s in range(2, 10):
                    slot(g, s, False)
            for s in range(2, 8):
                slot(NG - 1, s, True)

            def split_ffn(c, what, parity):
                n = {"gate": "q", "up": "k", "down": "o"}[what]
                split_lo(ffn_split(c, what), w[n][0][:, parity], w[n][1][:, parity], raw[n][:, parity])

            def scale_down(c, parity):
                pool.wait_ge(ffn_in["o"][parity], ffn_loaded(c, parity))
                pool.tensor_tensor(raw["o"][:, parity], raw["o"][:, parity], ad_sb, ALU.mult)\
                    .then_inc(wd_scaled, 1)

            pool.wait_ge(consts_in, 64)
            split_ffn(0, "gate", 0)
            split_ffn(0, "up", 0)
            scales(2, 0, False)
            scales(3, 1, False)

            def chunk(c, parity, more=True):
                scale_down(c, parity)
                if more:
                    split_ffn(c + 1, "gate", 1 - parity)
                    split_ffn(c + 1, "up", 1 - parity)
                    split_ffn(c, "down", parity)
                else:
                    split_lo(c * 3 + (ATT_SPLITS + 3), w["o"][0][:, parity], w["o"][1][:, parity],
                             raw["o"][:, parity])

            chunk(0, 0)
            with pool.Fori(0, (FC - 3) // 2, 1) as j:
                chunk(j * 2 + 1, 1)
                chunk(j * 2 + 2, 0)
            chunk(FC - 2, 1)
            chunk(FC - 1, 0, False)

        def evacuated(kind, h, half):
            if kind == "v":
                return v[:, 2 * h:2 * h + 2, :].rearrange("p b n -> p (b n)")
            return (q if kind == "q" else k)[:, h, half * HALF:(half + 1) * HALF]

        def step_dest(key):
            what, s = key
            if what == "A":
                return evacuated(*a_kind(s))
            return evacuated("v", V_PAIR.get(s if s >= 2 else s + 8), 0)

        @block.scalar
        def _(act):
            act.wait_ge(pool_init, 3)
            act.activation(warm[:, :], minus_half[:, 0:1], ACT.Exp).then_inc(pool_init, 1)

            def split_hi(hi, source):
                act.activation(hi, source, ACT.Copy).then_inc(w_hi, 1)

            def split_att(key):
                n, h = key
                part = (slice(None), h) if n in "qk" else (slice(None), slice(None))
                split_hi(w[n][0][part], raw[n][part])

            def split_c(half):
                for j in range(2):
                    act.wait_ge(c_in[j], 16 * (half + 1))
                    act.activation(cT[0][:, 2 * j:2 * j + 2, half * HALF:(half + 1) * HALF],
                                   cstage[j], ACT.Copy)\
                        .then_inc(c_hi, 1)

            def turn_hi(n, half, scaled):
                for c in range(DC):
                    act.wait_ge(turned, DC * n + c + 1)
                    dst = xT[0][:, c, half * HALF:(half + 1) * HALF]
                    if scaled:
                        act.activation(dst, bank[TURN[c % 2]][:, :], ACT.Copy, scale=lnw_sb[:, c:c + 1])\
                            .then_inc(turned_hi, 1)
                    else:
                        act.activation(dst, bank[TURN[c % 2]][:, :], ACT.Copy).then_inc(turned_hi, 1)

            def proj(n, b, dst):
                act.wait_ge(proj_done, n + 1)
                act.activation(dst, bank[b][:, :], ACT.Copy).then_inc(proj_ready, 1)

            split_c(0)
            act.wait_ge(w_in["k"], 16)
            split_att(("k", 0))
            split_att(("k", 1))
            act.wait_ge(w_in["v"], 16)
            split_att(("v", 0))
            act.wait_ge(w_in["q"], 16)
            split_att(("q", 0))
            split_att(("q", 1))
            for n, (kind, h) in enumerate(PRO[:4]):
                proj(n, n % NB, evacuated(kind, h, 0))
            act.wait_ge(consts_in, 16)
            turn_hi(0, 0, True)
            for n in (4, 5):
                proj(n, n % NB, evacuated(PRO[n][0], PRO[n][1], 0))
            split_c(1)
            turn_hi(1, 1, True)

            def softmax_exp(n):
                act.wait_ge(max_ready, n + 1)
                if not isinstance(n, int) or n > 0:
                    act.wait_ge(pt_done, n)
                for h in range(GH):
                    ins = act.activation(pr[:, h, :], sc[:, h, :], ACT.Exp, bias=negmax[:, h:h + 1],
                                         scale=1.0, accum_out=rowsum[:, h:h + 1])
                ins.then_inc(exp_done, 1)

            def at_part(n, b):
                act.wait_ge(pv_done, n + 1)
                act.activation(at[0][:, b % HB, :], PV_BANK[:, 0:GH * S], ACT.Copy).then_inc(at_hi, 1)

            def pt_part(n):
                act.wait_ge(pt_done, n + 1)
                act.activation(pt[:, :, :].rearrange("p h n -> p (h n)"), T_BANK[:, 0:GH * S], ACT.Copy)\
                    .then_inc(pt_ready, 1)

            for s in range(2):
                if s == 1:
                    proj(7, 7 % NB, step_dest(("V", 0)))
                softmax_exp(s)
                n = 6 if s == 0 else 8
                proj(n, n % NB, step_dest(("A", s)))
                if s == 1:
                    at_part(0, 0)
                pt_part(s)

            def weights(g, s, last):
                for n in SPLIT_OF.get(s, []):
                    if last and n > 0:
                        continue
                    kind, h = SPLITS[n]
                    if kind == "o":
                        act.wait_ge(w_in["o"], g * 16 + 16)
                        if not isinstance(g, int) or g > 0:
                            act.wait_ge(o_done, g * B)
                    elif kind == "v":
                        act.wait_ge(w_in["v"], g * 16 + 32)
                        act.wait_ge(proj_done, ring_step(g, ("V", 2)) + 1)
                    else:
                        act.wait_ge(w_in[kind], g * 16 + 32)
                        used = {("q", 0): 0, ("k", 0): 1, ("q", 1): 2, ("k", 1): 3}[(kind, h)]
                        if used >= 2:
                            act.wait_ge(proj_done, ring_step(g, ("A", used)) + 1)
                        else:
                            act.wait_ge(proj_done, ring_step(g, ("A", 2)) - (3 if used == 0 else 1) + 1)
                    split_att(SPLITS[n])

            def slot(g, s, last):
                if s - 1 in V_PAIR and not (last and s - 1 > 2):
                    n = ring_step(g, ("V", s - 1))
                    proj(n, ring_bank(("V", s - 1)), step_dest(("V", s - 1)))
                if not (last and s >= B):
                    softmax_exp(g * B + s)
                if s == 2 and not (isinstance(g, int) and g == 0):
                    weights(g, s, last)
                if not (last and s >= 4):
                    proj(ring_step(g, ("A", s)), ring_bank(("A", s)), step_dest(("A", s)))
                if not (last and s > B):
                    at_part(g * B + s - 1, (s - 1) % B)
                if not (last and s >= B):
                    pt_part(g * B + s)
                if s != 2 or (isinstance(g, int) and g == 0):
                    weights(g, s, last)

            for s in range(2, 10):
                slot(0, s, False)
            with act.Fori(1, NG - 1, 1) as g:
                for s in range(2, 10):
                    slot(g, s, False)
            for s in range(2, 9):
                slot(NG - 1, s, True)

            def ffn_weights(c, what, parity):
                n = {"gate": "q", "up": "k", "down": "o"}[what]
                if what == "down":
                    act.wait_ge(wd_scaled, c + 1)
                else:
                    act.wait_ge(ffn_in[n][parity], ffn_loaded(c, parity))
                split_hi(w[n][0][:, parity], raw[n][:, parity])

            ffn_weights(0, "gate", 0)
            ffn_weights(0, "up", 0)
            turn_hi(2, 0, False)
            turn_hi(3, 1, False)

            def silu(c, parity, half):
                act.wait_ge(gate_done, c * 2 + half + 1)
                if not isinstance(c, int) or c > 0:
                    act.wait_ge(h_ready, c * 2 + (half - 1))
                act.activation(nrm[:, half, :], GATE[half][:, :], ACT.Silu, scale=ag_now[:, parity:parity + 1])\
                    .then_inc(silu_done, 1)

            def hidden_hi(c, parity, half):
                act.wait_ge(h_ready, c * 2 + half + 1)
                act.activation(hid[0][:, parity, half * HALF:(half + 1) * HALF], nrm[:, 2 + half, :], ACT.Copy)\
                    .then_inc(h_hi, 1)

            def chunk(c, parity, more=True):
                act.activation(ag_now[:, parity:parity + 1], ag_sb[:, bass.ds(c, 1)], ACT.Copy)\
                    .then_inc(ag_set, 1)
                act.wait_ge(ag_set, c + 1)
                silu(c, parity, 0)
                if more:
                    ffn_weights(c + 1, "gate", 1 - parity)
                    ffn_weights(c + 1, "up", 1 - parity)
                hidden_hi(c, parity, 0)
                ffn_weights(c, "down", parity)
                silu(c, parity, 1)
                hidden_hi(c, parity, 1)

            chunk(0, 0)
            with act.Fori(0, (FC - 3) // 2, 1) as j:
                chunk(j * 2 + 1, 1)
                chunk(j * 2 + 2, 0)
            chunk(FC - 2, 1)
            chunk(FC - 1, 0, False)

        @block.vector
        def _(dve):
            def row_stats(n, half, ready):
                for b in range(half * HB, (half + 1) * HB):
                    ready(b)
                    dve.bn_stats(stats[:, b, :], y[:, b, :]).then_inc(stats_set, 1)
                for b in range(half * HB, (half + 1) * HB):
                    dve.wait_ge(stats_set, HB * n + b % HB + 1)
                    ins = dve.bn_aggr(mv[:, b, :], stats[:, b, :])
                ins.then_inc(stats_ready, 1)

            def normalise(n, half, residual):
                dve.wait_ge(scale_ready, n + 1)
                if n > 0:
                    dve.wait_ge(turned, DC * n)
                for b in range(half * HB, (half + 1) * HB):
                    dve.tensor_scalar(nrm[:, b % HB, :], y[:, b, :], mv[:, b, 0:1], small[:, 0, b:b + 1],
                                      ALU.subtract, ALU.mult).then_inc(nrm_ready, 1)
                if residual:
                    for b in range(half * HB, (half + 1) * HB):
                        dve.tensor_scalar(y[:, b, :], y[:, b, :], small[:, 1, b:b + 1], small[:, 2, b:b + 1],
                                          ALU.mult, ALU.add).then_inc(residual_set, 1)

            def turn_lo(n, half, scaled):
                for c in range(DC):
                    dve.wait_ge(turned_hi, DC * n + c + 1)
                    part = (slice(None), c, slice(half * HALF, (half + 1) * HALF))
                    if scaled:
                        dve.scalar_tensor_tensor(xT[1][part], bank[TURN[c % 2]][:, :], lnw_sb[:, c:c + 1],
                                                 xT[0][part], ALU.mult, ALU.subtract).then_inc(turned_lo, 1)
                    else:
                        dve.tensor_tensor(xT[1][part], bank[TURN[c % 2]][:, :], xT[0][part], ALU.subtract)\
                            .then_inc(turned_lo, 1)

            def c_part(half):
                for j in range(2):
                    dve.wait_ge(c_hi, 2 * half + j + 1)
                    part = (slice(None), slice(2 * j, 2 * j + 2), slice(half * HALF, (half + 1) * HALF))
                    dve.tensor_tensor(cT[1][part], cstage[j],
                                      cT[0][part], ALU.subtract).then_inc(c_lo, 1)

            dve.memset(rowsum[:, :], 0.0).then_inc(y_added, O_FREE)
            dve.memset(rinv[:, :], 0.0).then_inc(y2_added, DOWN_FREE)
            c_part(0)
            row_stats(0, 0, lambda b: dve.wait_ge(x_in[0], 16 * HB))
            row_stats(1, 1, lambda b: dve.wait_ge(x_in[1], 16 * HB))
            normalise(0, 0, True)
            dve.wait_ge(consts_in, 16)
            turn_lo(0, 0, True)
            normalise(1, 1, True)
            c_part(1)
            dve.wait_ge(mask_in, 16)
            dve.tensor_scalar(maskadd[:, :, :], mask_u8[:, :, :], -MASKED, MASKED, ALU.mult, ALU.add)\
                .then_inc(mask_ready, 1)
            dve.tensor_reduce(some[:, :], mask_u8[:, :, :], AX.X, ALU.max).then_inc(mask_set, 1)
            turn_lo(1, 1, True)
            dve.wait_ge(mask_set, 1)

            def scores(n, b):
                dve.wait_ge(scores_done, n + 1)
                dve.wait_ge(bm_ready, n + 1)
                dve.tensor_tensor(sc[:, :, :].rearrange("p h n -> p (h n)"), S_BANK[:, 0:GH * S],
                                  bm[:, b % 4, :, :].rearrange("p h n -> p (h n)"), ALU.add)\
                    .then_inc(masked_ready, 1)
                dve.wait_ge(masked_ready, n + 1)
                dve.tensor_reduce(negmax[:, :], sc[:, :, :], AX.X, ALU.max, negate=True).then_inc(max_ready, 1)

            def probs(n, b):
                dve.wait_ge(exp_done, n + 1)
                dve.reciprocal(rinv[:, :], rowsum[:, :]).then_inc(rinv_ready, 1)
                dve.wait_ge(rinv_ready, n + 1)
                for h in range(GH):
                    ins = dve.tensor_scalar(pr[:, h, :], pr[:, h, :], rinv[:, h:h + 1], some[:, b:b + 1],
                                            ALU.mult, ALU.mult)
                ins.then_inc(prob_ready, 1)

            def at_part(n, b):
                dve.wait_ge(at_hi, n + 1)
                dve.tensor_tensor(at[1][:, b % HB, :], PV_BANK[:, 0:GH * S], at[0][:, b % HB, :], ALU.subtract)\
                    .then_inc(at_lo, 1)

            def add_out(n, b):
                dve.wait_ge(o_done, n + 1)
                dve.tensor_tensor(y[:, b, :], O_BANK[b % 2][:, :], y[:, b, :], ALU.add).then_inc(y_added, 1)

            for s in range(2):
                scores(s, s)
                probs(s, s)
                if s == 1:
                    at_part(0, 0)

            def slot(g, s, last):
                if not (last and s >= B):
                    scores(g * B + s, s % B)
                if not (last and s >= B):
                    probs(g * B + s, s % B)
                for b in O_OF[s]:
                    add_out(g * B + b, b)
                if not (last and s > B):
                    at_part(g * B + s - 1, (s - 1) % B)

            with dve.Fori(0, NG - 1, 1) as g:
                for s in range(2, 10):
                    slot(g, s, False)
            for s in range(2, 8):
                slot(NG - 1, s, True)

            def complete(b):
                dve.wait_ge(y_added, (NG - 1) * B + b + 1 + O_FREE)

            row_stats(2, 0, complete)
            normalise(2, 0, False)
            slot(NG - 1, 8, True)
            turn_lo(2, 0, False)
            slot(NG - 1, 9, True)
            row_stats(3, 1, complete)
            normalise(3, 1, False)
            turn_lo(3, 1, False)

            def hidden(c, half):
                dve.wait_ge(up_done, c * 2 + half + 1)
                dve.wait_ge(silu_done, c * 2 + half + 1)
                if isinstance(c, int) and c == 0:
                    dve.wait_ge(turned, DC * 4)
                dve.scalar_tensor_tensor(nrm[:, 2 + half, :], UP[half][:, :], au_sb[:, bass.ds(c, 1)],
                                         nrm[:, half, :], ALU.mult, ALU.mult).then_inc(h_ready, 1)

            def hidden_lo(c, parity, half):
                dve.wait_ge(h_hi, c * 2 + half + 1)
                part = (slice(None), parity, slice(half * HALF, (half + 1) * HALF))
                dve.tensor_tensor(hid[1][part], nrm[:, 2 + half, :], hid[0][part], ALU.subtract).then_inc(h_lo, 1)

            def add_down(c, b):
                dve.wait_ge(down_done, c * B + b + 1)
                dve.tensor_tensor(y[:, b, :], DOWN[b % 4][:, :], y[:, b, :], ALU.add).then_inc(y2_added, 1)

            def chunk(c, parity, first=False):
                for half in range(2):
                    hidden(c, half)
                    if not first:
                        for b in range(half * HB, (half + 1) * HB):
                            add_down(c - 1, b)
                    hidden_lo(c, parity, half)

            chunk(0, 0, True)
            with dve.Fori(0, (FC - 1) // 2, 1) as j:
                chunk(j * 2 + 1, 1)
                chunk(j * 2 + 2, 0)
            for b in range(B):
                add_down(FC - 1, b)

        @block.tensor
        def _(pe):
            PARTS = [(0, 0), (0, 1), (1, 0)]

            def product(dst, terms):
                total = len(terms) * len(PARTS)
                n = 0
                for stationary, moving in terms:
                    for i, j in PARTS:
                        mm = pe.matmul(dst, stationary(i), moving(j), start=(n == 0), stop=(n == total - 1))
                        n += 1
                return mm

            def turn(n, half):
                for c in range(DC):
                    if n or c >= 2:
                        pe.wait_ge(turned_lo, DC * n + c - 1)
                    if c == 0:
                        pe.wait_ge(nrm_ready, HB * (n + 1))
                    for i in range(HB):
                        mm = pe.transpose(bank[TURN[c % 2]][:, i * S:(i + 1) * S], nrm[:, i, c * P:(c + 1) * P],
                                          ident[:, :])
                    mm.then_inc(turned, 1)

            def project(bk, kind, h, half):
                src, wt = (xT if kind == "q" else cT), w[kind]
                return product(bank[bk][:, :], [
                    (lambda i, c=c: wt[i][:, h, c * P:(c + 1) * P],
                     lambda j, c=c: src[j][:, c, half * HALF:(half + 1) * HALF]) for c in range(DC)])

            def project_v(bk, pair):
                wt = [w["v"][i][:, :, :].rearrange("p a b -> p (a b)") for i in range(2)]
                for e in range(2):
                    b = 2 * pair + e
                    mm = product(bank[bk][:, e * GH * DH:(e + 1) * GH * DH], [
                        (lambda i, c=c: cT[i][:, c, b * S:(b + 1) * S],
                         lambda j, c=c: wt[j][:, c * GH * DH:(c + 1) * GH * DH]) for c in range(DC)])
                return mm

            def scores(n, b):
                if not isinstance(n, int) or n > 0:
                    pe.wait_ge(masked_ready, n)
                t = slice(b * S, (b + 1) * S)
                for h in range(GH):
                    mm = pe.matmul(S_BANK[:, h * S:(h + 1) * S], q[:, h, t], k[:, h, t], start=True, stop=True)
                mm.then_inc(scores_done, 1)

            def turn_probs(n):
                pe.wait_ge(prob_ready, n + 1)
                if not isinstance(n, int) or n > 0:
                    pe.wait_ge(pt_ready, n)
                for h in range(GH):
                    mm = pe.transpose(T_BANK[:, h * S:(h + 1) * S], pr[:, h, :], ident[:, :])
                mm.then_inc(pt_done, 1)

            def values(n, b):
                pe.wait_ge(pt_ready, n + 1)
                if not isinstance(n, int) or n > 0:
                    pe.wait_ge(at_lo, n)
                for h in range(GH):
                    mm = pe.matmul(PV_BANK[:, h * S:(h + 1) * S], v[:, b, h * DH:(h + 1) * DH], pt[:, h, :],
                                   start=True, stop=True)
                mm.then_inc(pv_done, 1)

            def output(n, b):
                pe.wait_ge(at_lo, n + 1)
                pe.wait_ge(y_added, n + 1)
                product(O_BANK[b % 2][:, :], [
                    (lambda i, h=h: at[i][:, b % HB, h * S:(h + 1) * S],
                     lambda j, h=h: w["o"][j][:, h, :]) for h in range(GH)]).then_inc(o_done, 1)

            pe.wait_ge(pool_init, 3)
            pe.wait_ge(c_lo, 2)
            for n in range(4):
                kind, h = PRO[n]
                pe.wait_ge(w_lo, min(n + 1, 3))
                if n >= NB:
                    pe.wait_ge(proj_ready, n - NB + 1)
                (project(n % NB, kind, h, 0) if kind == "k" else project_v(n % NB, h)).then_inc(proj_done, 1)
            pe.wait_ge(proj_ready, 4)
            turn(0, 0)
            pe.wait_ge(turned_lo, 4)
            pe.wait_ge(w_lo, 5)
            for n in (4, 5):
                project(n % NB, "q", PRO[n][1], 0).then_inc(proj_done, 1)
            pe.wait_ge(proj_ready, 6)
            turn(1, 1)
            scores(0, 0)
            pe.wait_ge(turned_lo, 8)
            pe.wait_ge(c_lo, 4)

            def proj_step(g, key):
                what, s = key
                n = ring_step(g, key)
                pe.wait_ge(proj_ready, n - (NB - 1))
                if what == "A":
                    mm = project(ring_bank(key), *a_kind(s))
                else:
                    mm = project_v(ring_bank(key), V_PAIR[s])
                mm.then_inc(proj_done, 1)

            for s in range(2):
                n = 6 if s == 0 else 8
                pe.wait_ge(proj_ready, n - (NB - 1))
                project(n % NB, *a_kind(s)).then_inc(proj_done, 1)
                if s == 1:
                    values(0, 0)
                turn_probs(s)
                if s == 0:
                    project_v(7 % NB, V_PAIR[8]).then_inc(proj_done, 1)
                scores(s + 1, s + 1)

            def slot(g, s, last):
                if not (last and s >= 4):
                    if 4 <= s < 8:
                        n = SPLITS.index(a_kind(s)[0:2])
                        pe.wait_ge(w_lo, split_count(g, n))
                    proj_step(g, ("A", s))
                for b in O_OF[s]:
                    if b == 0:
                        pe.wait_ge(w_lo, split_count(g, 0))
                    output(g * B + b, b)
                if not (last and s > B):
                    values(g * B + s - 1, (s - 1) % B)
                if not (last and s >= B):
                    turn_probs(g * B + s)
                if s in V_PAIR and not (last and s > 2):
                    if s == 5:
                        pe.wait_ge(w_lo, split_count(g, 2))
                    proj_step(g, ("V", s))
                if not (last and s >= B - 1):
                    if s in (3, 7):
                        pe.wait_ge(proj_ready, ring_step(g, ("A", s)) + 1)
                    scores(g * B + s + 1, (s + 1) % B)

            with pe.Fori(0, NG - 1, 1) as g:
                for s in range(2, 10):
                    slot(g, s, False)
            for s in range(2, 10):
                slot(NG - 1, s, True)
                if s == 8:
                    turn(2, 0)
            turn(3, 1)

            def gate_up(c, parity, half):
                cols = slice(half * HALF, (half + 1) * HALF)
                for n, dst, done in (("q", GATE, gate_done), ("k", UP, up_done)):
                    if not isinstance(c, int) or c > 0:
                        pe.wait_ge(h_ready, c * 2 + (half - 1))
                    if half == 0:
                        pe.wait_ge(w_lo, ffn_split(c, "gate" if n == "q" else "up"))
                    product(dst[half][:, :], [
                        (lambda i, c_=c_: w[n][i][:, parity, c_ * P:(c_ + 1) * P],
                         lambda j, c_=c_: xT[j][:, c_, cols]) for c_ in range(DC)]).then_inc(done, 1)

            def down(c, parity, b):
                if b % HB == 0:
                    pe.wait_ge(h_lo, c * 2 + b // HB + 1)
                if b == 0:
                    pe.wait_ge(w_lo, (c * 3 + (ATT_SPLITS + 3)) if isinstance(c, int) and c == FC - 1
                               else ffn_split(c, "down"))
                pe.wait_ge(y2_added, c * B + b + 1)
                product(DOWN[b % 4][:, :], [
                    (lambda i: hid[i][:, parity, b * S:(b + 1) * S],
                     lambda j: w["o"][j][:, parity, :])]).then_inc(down_done, 1)

            def chunk(c, parity, first=False):
                for half in range(2):
                    if first:
                        pe.wait_ge(turned_lo, DC * (3 + half))
                    gate_up(c, parity, half)
                    if not first:
                        for b in range(half * HB, (half + 1) * HB):
                            down(c - 1, 1 - parity, b)

            chunk(0, 0, True)
            with pe.Fori(0, (FC - 1) // 2, 1) as j:
                chunk(j * 2 + 1, 1)
                chunk(j * 2 + 2, 0)
            for b in range(B):
                down(FC - 1, 0, b)


def kernel(**inputs):
    import numpy as np
    import concourse.bacc as bacc
    from concourse.bass_utils import run_bass_kernel_spmd as run

    def a(name):
        return np.asarray(inputs[name])

    def pad(m, axis):
        shape = list(m.shape)
        shape[axis] = FC * P - FF
        return np.concatenate([m, np.zeros(shape, m.dtype)], axis=axis)

    def by_head(m):
        return m.reshape(NG, GH, DH, DC, P).transpose(0, 4, 1, 3, 2).reshape(NG, P, GH * D)

    layouts = {
        "x": a("x"),
        "ctxt": a("ctx_4096").reshape(T, DC, P).transpose(2, 1, 0),
        "mask": a("mask_BxSxS2_bk0").transpose(1, 0, 2),
        "bias": a("L0_xattn_position_bias").reshape(NG, GH, S, S).transpose(0, 2, 1, 3).reshape(NG, S, GH * S),
        "lnw": a("L0_xattn_ln_weight").reshape(DC, P).T,
        "wq": by_head(a("L0_xattn_w_q")),
        "wk": by_head(a("L0_xattn_w_k")),
        "wv": a("L0_xattn_w_v").reshape(NG, GH * DH, DC, P).transpose(0, 3, 2, 1).reshape(NG, P, GH * D),
        "wo": a("L0_xattn_w_out").reshape(D, NG, GH, DH).transpose(1, 3, 2, 0).reshape(NG, P, GH * D),
        "wg": pad(a("L0_ffn_Wg"), 0).reshape(FC, P, DC, P).transpose(0, 3, 2, 1).reshape(FC, P, D),
        "wu": pad(a("L0_ffn_Wu"), 0).reshape(FC, P, DC, P).transpose(0, 3, 2, 1).reshape(FC, P, D),
        "wd": pad(a("L0_ffn_Wd"), 1).reshape(D, FC, P).transpose(1, 2, 0),
        "ag": pad(a("L0_ffn_ag"), 0).reshape(FC, P).T,
        "au": pad(a("L0_ffn_au"), 0).reshape(FC, P).T,
        "ad": a("L0_ffn_ad"),
    }
    nc = bacc.Bacc("TRN2", target_bir_lowering=False, num_devices=1)
    arrays, args = {}, []
    for name, m in layouts.items():
        m = np.ascontiguousarray(m)
        arrays[f"in_{name}"] = m
        args.append(nc.dram_tensor(f"in_{name}", m.shape, mybir.dt.from_np(m.dtype), kind="ExternalInput").ap())
    args.append(nc.dram_tensor("out_0", (B, S, D), mybir.dt.float32, kind="ExternalOutput").ap())
    program(nc, *args)
    return run(nc, [arrays], core_ids=[0]).results[0]["out_0"]
```

```python
import concourse.bass as bass
from concourse import mybir
from contextlib import ExitStack

B, S, D, H, DH = 8, 128, 512, 32, 128
P = 128
T = B * S
DC = D // P
GH = 2
NG = H // GH
HALF = T // 2
HB = B // 2
FF = 1376
FC = -(-FF // P)
EPS = 1e-5
CHECK = FC * P * D // (P * NG)
MASKED = -1e30

PRO = [("k", 0), ("k", 1), ("v", 0), ("v", 1), ("q", 0), ("q", 1), ("A", 0), ("V", 0), ("A", 1)]
RING = [("A", 2), ("V", 2), ("A", 3), ("A", 4), ("A", 5), ("V", 5), ("A", 6), ("V", 6), ("A", 7),
        ("A", 8), ("V", 8), ("A", 9)]
NB = 3
V_PAIR = {2: 3, 5: 0, 6: 1, 8: 2}
O_OF = {2: [], 3: [0], 4: [1, 2], 5: [3], 6: [4], 7: [5], 8: [6], 9: [7]}
SPLIT_PRO = [("k", 0), ("k", 1), ("v", 0), ("q", 0), ("q", 1)]
SPLITS = [("o", 0), ("q", 0), ("v", 0), ("k", 0), ("q", 1), ("k", 1)]
SPLIT_OF = {2: [0, 1], 3: [2, 3], 4: [4], 5: [5]}


def ring_step(g, key):
    return g * len(RING) + (len(PRO) + RING.index(key))


def ring_bank(key):
    return RING.index(key) % NB


def a_kind(s):
    return "qkqk"[s % 4], (s % 4) // 2, 1 if s % 8 < 4 else 0


def split_count(g, n):
    return g * len(SPLITS) + (len(SPLIT_PRO) + n + 1)


def program(nc, x, ctxt, mask, bias, lnw, wq, wk, wv, wo, wg, wu, wd, ag, au, ad, out):
    f32 = mybir.dt.float32
    f32r = mybir.dt.float32r
    u8 = mybir.dt.uint8
    ALU = mybir.AluOpType
    ACT = mybir.ActivationFunctionType
    AX = mybir.AxisListType

    ctx = ExitStack()
    with ctx:
        def sb(name, shape, dt=f32):
            return ctx.enter_context(nc.sbuf_tensor(name, shape, dt))

        inner = ExitStack()

        def phase(name, shape, dt=f32):
            return inner.enter_context(nc.sbuf_tensor(name, shape, dt))

        def sem(name):
            return ctx.enter_context(nc.semaphore(name))

        xT = [sb("xT_hi", [P, DC, T], f32r), sb("xT_lo", [P, DC, T], f32r)]
        cT = [sb("cT_hi", [P, DC, T], f32r), sb("cT_lo", [P, DC, T], f32r)]
        y = sb("y", [P, B, D])
        at = [sb("at_hi", [P, HB, GH * S], f32r), sb("at_lo", [P, HB, GH * S], f32r)]
        raw = {n: sb(f"w{n}_raw", [P, GH, D]) for n in "qkvo"}
        w = {n: [sb(f"w{n}_hi", [P, GH, D], f32r), sb(f"w{n}_lo", [P, GH, D], f32r)] for n in "qkvo"}
        bias_sb = sb("bias_sb", [P, GH, S])
        maskadd = sb("maskadd", [P, B, S])
        ad_sb = maskadd[:, 0:D // S, :].rearrange("p b n -> p (b n)")
        some = sb("some", [P, B])
        bm = sb("bm", [P, 4, GH, S])
        sc = sb("sc", [P, GH, S])
        pr = sb("pr", [P, GH, S])
        pt = sb("pt", [P, GH, S])
        negmax = sb("negmax", [P, GH])
        rowsum = sb("rowsum", [P, GH])
        rinv = sb("rinv", [P, GH])
        ident = sb("ident", [P, P])
        nrm = sb("nrm", [P, HB, D])
        cstage = [raw["o"][:, :, :], bm[:, :, :, :].rearrange("p r h n -> p (r h) n")\
                  .rearrange("p (a r) n -> p a (r n)", a=2)]
        nrm_flat = nrm[:, :, :].rearrange("p b n -> p (b n)")
        checked = nrm_flat[:, 0:3 * CHECK]
        low_halves = checked.bitcast(mybir.dt.uint16).rearrange("p (n e) -> p n e", e=2)[:, :, 0]
        check_junk = nrm_flat[:, 3 * CHECK:3 * CHECK + 3 * CHECK // 2].bitcast(mybir.dt.bfloat16)
        stats = sb("stats", [P, B, 6])
        mv = sb("mv", [P, B, 2])
        small = sb("small", [P, 8, B])
        minus_half = sb("minus_half", [P, B])
        lnw_sb = sb("lnw_sb", [P, DC])
        ag_sb = sb("ag_sb", [P, FC])
        au_sb = sb("au_sb", [P, FC])
        low_now = sb("low_now", [P, 1])
        low_sum = sb("low_sum", [P, 1])
        lo_used = sb("lo_used", [1, 1], mybir.dt.int32)
        ones = sb("ones", [P, 1])
        ag_now = sb("ag_now", [P, 2])
        mask_u8 = sb("mask_u8", [P, B, S], u8)
        warm = sb("warm", [P, 1])

        q = phase("q", [P, GH, T])
        k = phase("k", [P, GH, T])
        v = phase("v", [P, B, GH * DH])
        inner.close()
        hid = [phase("hid_hi", [P, 2, T], f32r), phase("hid_lo", [P, 2, T], f32r)]
        y2 = phase("y2", [P, B, D])
        ctx.enter_context(inner)

        bank = [ctx.enter_context(nc.psum_tensor(f"bank{i}", [P, 512], f32)) for i in range(8)]
        S_BANK, T_BANK, PV_BANK, O_BANK = bank[3], bank[4], bank[5], bank[6:8]
        TURN = [bank[4:8], bank[0:4]]
        O_FREE, DOWN_FREE = 2, 4
        GATE, UP, DOWN = [bank[4], bank[6]], [bank[5], bank[7]], bank[0:4]
        FLAG = GATE[0]

        x_in = [sem(f"x_in{i}") for i in range(2)]
        c_in = [sem(f"c_in{i}") for i in range(2)]
        consts_in = sem("consts_in")
        mask_in = sem("mask_in")
        w_in = {n: sem(f"w{n}_in") for n in "qkvo"}
        ffn_in = {n: [sem(f"ffn_w{n}_in{i}") for i in range(2)] for n in "qko"}
        bias_in = sem("bias_in")
        pool_init = sem("pool_init")
        mask_set = sem("mask_set")
        mask_ready = sem("mask_ready")
        stats_set = sem("stats_set")
        residual_set = sem("residual_set")
        stats_ready = sem("stats_ready")
        scale_step = sem("scale_step")
        scale_ready = sem("scale_ready")
        nrm_ready = sem("nrm_ready")
        turned = sem("turned")
        turned_hi = sem("turned_hi")
        turned_lo = sem("turned_lo")
        c_hi = sem("c_hi")
        c_lo = sem("c_lo")
        w_hi = sem("w_hi")
        w_lo = sem("w_lo")
        proj_done = sem("proj_done")
        proj_ready = sem("proj_ready")
        bm_ready = sem("bm_ready")
        scores_done = sem("scores_done")
        masked_ready = sem("masked_ready")
        max_ready = sem("max_ready")
        exp_done = sem("exp_done")
        rinv_ready = sem("rinv_ready")
        prob_ready = sem("prob_ready")
        pt_done = sem("pt_done")
        pt_ready = sem("pt_ready")
        pv_done = sem("pv_done")
        at_hi = sem("at_hi")
        at_lo = sem("at_lo")
        o_done = sem("o_done")
        y_added = sem("y_added")
        wd_scaled = sem("wd_scaled")
        ag_set = sem("ag_set")
        gate_done = sem("gate_done")
        up_done = sem("up_done")
        silu_done = sem("silu_done")
        h_ready = sem("h_ready")
        h_hi = sem("h_hi")
        h_lo = sem("h_lo")
        down_done = sem("down_done")
        check_in = sem("check_in")
        low_halves_summed = sem("low_halves_summed")
        low_added = sem("low_added")
        flag_done = sem("flag_done")
        flag_set = sem("flag_set")
        flag_seen = sem("flag_seen")
        merge_scaled = sem("merge_scaled")
        merged = sem("merged")
        y2_added = sem("y2_added")
        out_sent = sem("out_sent")

        block = ctx.enter_context(nc.Block())

        ATT_SPLITS = split_count(NG - 1, 0)

        def ffn_split(c, what):
            if what == "down":
                return c * 3 + (ATT_SPLITS + 5)
            return c * 3 + (ATT_SPLITS + (1 if what == "gate" else 2))

        def ffn_loaded(c, parity):
            return c * 8 + (16 - 8 * parity)

        LAST_SPLIT = ffn_split(FC - 2, "down") + 1

        @block.sync
        def _(sp):
            def load(n, source, g):
                src = source[bass.ds(g, 1), :, :].rearrange("o p n -> p (o n)")
                sp.dma_start(raw[n][:, :, :].rearrange("p h n -> p (h n)"), src).then_inc(w_in[n], 16)

            def load_bias(g):
                sp.dma_start(bias_sb[:, :, :].rearrange("p h n -> p (h n)"),
                             bias[bass.ds(g, 1), :, :].rearrange("o p n -> p (o n)")).then_inc(bias_in, 16)

            def load_c(half):
                for j in range(2):
                    sp.dma_start(cstage[j],
                                 ctxt[:, 2 * j:2 * j + 2, half * HALF:(half + 1) * HALF])\
                        .then_inc(c_in[j], 16)

            def load_x(half):
                for b in range(half * HB, (half + 1) * HB):
                    sp.dma_start(y[:, b, :], x[b, :, :]).then_inc(x_in[half], 16)

            load_c(0)
            load("k", wk, 0)
            load_x(0)
            load("v", wv, 0)
            sp.dma_start(lnw_sb[:, :], lnw).then_inc(consts_in, 16)
            load("q", wq, 0)
            load_x(1)
            sp.wait_ge(c_lo, 2)
            load_c(1)
            sp.dma_start(mask_u8[:, :, :], mask).then_inc(mask_in, 16)
            load_bias(0)
            sp.wait_ge(c_lo, 4)
            load("o", wo, 0)
            sp.dma_start(ag_sb[:, :], ag).then_inc(consts_in, 16)
            sp.dma_start(au_sb[:, :], au).then_inc(consts_in, 16)
            sp.wait_ge(w_lo, 3)
            load("k", wk, 1)
            load("v", wv, 1)
            sp.wait_ge(w_lo, len(SPLIT_PRO))
            load("q", wq, 1)

            def load_check(g):
                for i, source in enumerate((wg, wu, wd)):
                    flat = source.rearrange("c p n -> (c p n)").rearrange("(g p n) -> g p n", g=NG, p=P)
                    sp.dma_start(checked[:, i * CHECK:(i + 1) * CHECK],
                                 flat[bass.ds(g, 1), :, :].rearrange("o p n -> p (o n)")).then_inc(check_in, 16)

            sp.wait_ge(turned, 2 * DC)
            load_check(0)

            def attention_loads(g, more):
                sp.wait_ge(w_lo, split_count(g, 0))
                load("o", wo, g + 1)
                if more:
                    sp.wait_ge(w_lo, split_count(g, 2))
                    load("v", wv, g + 2)
                    sp.wait_ge(w_lo, split_count(g, 4))
                    load("q", wq, g + 2)
                    sp.wait_ge(w_lo, split_count(g, 5))
                    load("k", wk, g + 2)
                sp.wait_ge(bm_ready, g * B + B)
                load_bias(g + 1)
                sp.wait_ge(low_added, g + 2)
                load_check(g + 1)

            with sp.Fori(0, NG - 2, 1) as g:
                attention_loads(g, True)
            attention_loads(NG - 2, False)

            def load_ffn(n, source, c, parity):
                src = source[bass.ds(c, 1), :, :].rearrange("o p n -> p (o n)")
                sp.dma_start(raw[n][:, parity, :], src).then_inc(ffn_in[n][parity], 16)

            for c in range(2):
                if c == 0:
                    sp.wait_ge(w_lo, split_count(NG - 2, 5))
                load_ffn("q", wg, c, c)
                load_ffn("k", wu, c, c)
            sp.wait_ge(w_lo, ATT_SPLITS)
            sp.wait_ge(bm_ready, NG * B)
            sp.dma_start(ad_sb, ad.rearrange("(o n) -> o n", o=1).broadcast_to([P, D])).then_inc(consts_in, 16)
            load_ffn("o", wd, 0, 0)
            load_ffn("o", wd, 1, 1)

            def ffn_loads(c, parity):
                sp.wait_ge(w_lo, ffn_split(c + 1, "up"))
                load_ffn("q", wg, c + 3, 1 - parity)
                load_ffn("k", wu, c + 3, 1 - parity)
                sp.wait_ge(w_lo, ffn_split(c, "down"))
                load_ffn("o", wd, c + 2, parity)

            sp.wait_ge(w_lo, ffn_split(0, "up"))
            load_ffn("q", wg, 2, 0)
            load_ffn("k", wu, 2, 0)
            with sp.Fori(0, (FC - 3) // 2, 1) as j:
                ffn_loads(j * 2, 0)
                ffn_loads(j * 2 + 1, 1)
            sp.wait_ge(w_lo, ffn_split(FC - 3, "down"))
            load_ffn("o", wd, FC - 1, 0)
            for b in range(B):
                sp.wait_ge(merged, 2 * b + 2)
                sp.dma_start(out[b, :, :], y[:, b, :]).then_inc(out_sent, 16)
            sp.wait_ge(out_sent, 16 * B)

        @block.gpsimd
        def _(pool):
            pool.memset(ident[:, :], 0.0).then_inc(pool_init, 1)
            pool.memset(minus_half[:, :], -0.5).then_inc(pool_init, 1)
            pool.memset(ones[:, :], 1.0).then_inc(pool_init, 1)
            pool.memset(low_sum[:, :], 0.0).then_inc(low_added, 1)
            pool.wait_ge(pool_init, 3)
            pool.affine_select(out=ident[:, :], in_=ident[:, :], compare_op=ALU.not_equal, fill=1.0,
                               base=0, pattern=[[-1, P]], channel_multiplier=1).then_inc(pool_init, 1)
            pool.wait_ge(pool_init, 4)
            steps = [0]

            def link(ins):
                steps[0] += 1
                ins.then_inc(scale_step, 1)
                pool.wait_ge(scale_step, steps[0])

            def scales(n, half, rms):
                h = slice(half * HB, (half + 1) * HB)
                mean, var = mv[:, h, 0], mv[:, h, 1]
                pool.wait_ge(stats_ready, n + 1)
                link(pool.tensor_scalar(small[:, 3, h], var, EPS, 1.0, ALU.add, ALU.mult))
                if not rms:
                    pool.tensor_tensor(small[:, 0, h], small[:, 3, h], minus_half[:, h], ALU.pow)\
                        .then_inc(scale_ready, 1)
                    return
                link(pool.tensor_tensor(small[:, 4, h], small[:, 3, h], minus_half[:, h], ALU.pow))
                link(pool.tensor_tensor(small[:, 5, h], var, small[:, 4, h], ALU.mult))
                link(pool.tensor_tensor(small[:, 5, h], small[:, 5, h], small[:, 4, h], ALU.mult))
                link(pool.tensor_scalar(small[:, 5, h], small[:, 5, h], EPS, 1.0, ALU.add, ALU.mult))
                link(pool.tensor_tensor(small[:, 6, h], small[:, 5, h], minus_half[:, h], ALU.pow))
                link(pool.tensor_tensor(small[:, 0, h], small[:, 6, h], small[:, 4, h], ALU.mult))
                link(pool.tensor_scalar(small[:, 1, h], small[:, 4, h], 1.0, 1.0, ALU.add, ALU.mult))
                link(pool.tensor_tensor(small[:, 7, h], mean, small[:, 4, h], ALU.mult))
                pool.tensor_scalar(small[:, 2, h], small[:, 7, h], -1.0, 0.0, ALU.mult, ALU.add)\
                    .then_inc(scale_ready, 1)

            def split_lo(count, hi, lo, source):
                pool.wait_ge(w_hi, count)
                pool.tensor_tensor(lo, source, hi, ALU.subtract).then_inc(w_lo, 1)

            def split_att(count, key):
                n, h = key
                part = (slice(None), h) if n in "qk" else (slice(None), slice(None))
                split_lo(count, w[n][0][part], w[n][1][part], raw[n][part])

            def add_bias(n, b):
                pool.tensor_tensor(bm[:, b % 4, :, :], bias_sb[:, :, :],
                                   maskadd[:, b:b + 1, :].broadcast_to([P, GH, S]), ALU.add).then_inc(bm_ready, 1)

            for n in range(2):
                split_att(n + 1, SPLIT_PRO[n])
            scales(0, 0, True)
            for n in range(2, 5):
                split_att(n + 1, SPLIT_PRO[n])
            scales(1, 1, True)
            pool.wait_ge(mask_ready, 1)
            pool.wait_ge(bias_in, 16)
            pool.wait_ge(c_lo, 4)
            for b in range(4):
                add_bias(b, b)

            def slot(g, s, last):
                for n in SPLIT_OF.get(s, []):
                    if not last or n == 0:
                        split_att(split_count(g, n), SPLITS[n])
                if s + 2 < B or not last:
                    if s == 6:
                        pool.wait_ge(bias_in, g * 16 + 32)
                    pool.wait_ge(masked_ready, g * B + (s - 2 + 1))
                    add_bias(g * B + s + 2, (s + 2) % B)

            def add_low(g):
                pool.wait_ge(low_halves_summed, g + 1)
                pool.wait_ge(low_added, g + 1)
                pool.tensor_tensor(low_sum[:, :], low_sum[:, :], low_now[:, :], ALU.add).then_inc(low_added, 1)

            with pool.Fori(0, NG - 1, 1) as g:
                for s in range(2, 10):
                    slot(g, s, False)
                    if s == 8:
                        add_low(g)
            for s in range(2, 8):
                slot(NG - 1, s, True)
                if s == 4:
                    add_low(NG - 1)

            def split_ffn(c, what, parity):
                n = {"gate": "q", "up": "k", "down": "o"}[what]
                split_lo(ffn_split(c, what), w[n][0][:, parity], w[n][1][:, parity], raw[n][:, parity])

            scales(2, 0, False)
            split_ffn(0, "gate", 0)
            split_ffn(0, "up", 0)
            scales(3, 1, False)

            def chunk(c, parity):
                split_ffn(c + 1, "gate", 1 - parity)
                split_ffn(c + 1, "up", 1 - parity)
                split_ffn(c, "down", parity)

            chunk(0, 0)
            with pool.Fori(0, (FC - 3) // 2, 1) as j:
                chunk(j * 2 + 1, 1)
                chunk(j * 2 + 2, 0)
            chunk(FC - 2, 1)
            pool.wait_ge(consts_in, 64)
            pool.wait_ge(ffn_in["o"][0], ffn_loaded(FC - 1, 0))
            pool.tensor_tensor(raw["o"][:, 0], raw["o"][:, 0], ad_sb, ALU.mult).then_inc(wd_scaled, 1)
            split_lo(LAST_SPLIT, w["o"][0][:, 0], w["o"][1][:, 0], raw["o"][:, 0])
            for b in range(B):
                pool.wait_ge(y2_added, (FC - 2) * B + b + 1 + DOWN_FREE)
                pool.tensor_tensor(y2[:, b, :], y2[:, b, :], ad_sb, ALU.mult).then_inc(merge_scaled, 1)

        def evacuated(kind, h, half):
            if kind == "v":
                return v[:, 2 * h:2 * h + 2, :].rearrange("p b n -> p (b n)")
            return (q if kind == "q" else k)[:, h, half * HALF:(half + 1) * HALF]

        def step_dest(key):
            what, s = key
            if what == "A":
                return evacuated(*a_kind(s))
            return evacuated("v", V_PAIR.get(s if s >= 2 else s + 8), 0)

        @block.scalar
        def _(act):
            act.wait_ge(pool_init, 4)
            act.activation(warm[:, :], minus_half[:, 0:1], ACT.Exp).then_inc(pool_init, 1)

            def split_hi(hi, source):
                act.activation(hi, source, ACT.Copy).then_inc(w_hi, 1)

            def split_att(key):
                n, h = key
                part = (slice(None), h) if n in "qk" else (slice(None), slice(None))
                split_hi(w[n][0][part], raw[n][part])

            def split_c(half):
                for j in range(2):
                    act.wait_ge(c_in[j], 16 * (half + 1))
                    act.activation(cT[0][:, 2 * j:2 * j + 2, half * HALF:(half + 1) * HALF],
                                   cstage[j], ACT.Copy)\
                        .then_inc(c_hi, 1)

            def turn_hi(n, half, scaled):
                for c in range(DC):
                    act.wait_ge(turned, DC * n + c + 1)
                    dst = xT[0][:, c, half * HALF:(half + 1) * HALF]
                    if scaled:
                        act.activation(dst, TURN[0 if scaled else 1][c][:, :], ACT.Copy, scale=lnw_sb[:, c:c + 1])\
                            .then_inc(turned_hi, 1)
                    else:
                        act.activation(dst, TURN[0 if scaled else 1][c][:, :], ACT.Copy).then_inc(turned_hi, 1)

            def proj(n, b, dst):
                act.wait_ge(proj_done, n + 1)
                act.activation(dst, bank[b][:, :], ACT.Copy).then_inc(proj_ready, 1)

            split_c(0)
            act.wait_ge(w_in["k"], 16)
            split_att(("k", 0))
            split_att(("k", 1))
            act.wait_ge(w_in["v"], 16)
            split_att(("v", 0))
            act.wait_ge(w_in["q"], 16)
            split_att(("q", 0))
            split_att(("q", 1))
            for n, (kind, h) in enumerate(PRO[:4]):
                proj(n, n % NB, evacuated(kind, h, 0))
            act.wait_ge(consts_in, 16)
            turn_hi(0, 0, True)
            for n in (4, 5):
                proj(n, n % NB, evacuated(PRO[n][0], PRO[n][1], 0))
            split_c(1)
            turn_hi(1, 1, True)

            def softmax_exp(n):
                act.wait_ge(max_ready, n + 1)
                if not isinstance(n, int) or n > 0:
                    act.wait_ge(pt_done, n)
                for h in range(GH):
                    ins = act.activation(pr[:, h, :], sc[:, h, :], ACT.Exp, bias=negmax[:, h:h + 1],
                                         scale=1.0, accum_out=rowsum[:, h:h + 1])
                ins.then_inc(exp_done, 1)

            def at_part(n, b):
                act.wait_ge(pv_done, n + 1)
                act.activation(at[0][:, b % HB, :], PV_BANK[:, 0:GH * S], ACT.Copy).then_inc(at_hi, 1)

            def pt_part(n):
                act.wait_ge(pt_done, n + 1)
                act.activation(pt[:, :, :].rearrange("p h n -> p (h n)"), T_BANK[:, 0:GH * S], ACT.Copy)\
                    .then_inc(pt_ready, 1)

            for s in range(2):
                if s == 1:
                    proj(7, 7 % NB, step_dest(("V", 0)))
                softmax_exp(s)
                n = 6 if s == 0 else 8
                proj(n, n % NB, step_dest(("A", s)))
                if s == 1:
                    at_part(0, 0)
                pt_part(s)

            def weights(g, s, last):
                for n in SPLIT_OF.get(s, []):
                    if last and n > 0:
                        continue
                    kind, h = SPLITS[n]
                    if kind == "o":
                        act.wait_ge(w_in["o"], g * 16 + 16)
                        if not isinstance(g, int) or g > 0:
                            act.wait_ge(o_done, g * B)
                    elif kind == "v":
                        act.wait_ge(w_in["v"], g * 16 + 32)
                        act.wait_ge(proj_done, ring_step(g, ("V", 2)) + 1)
                    else:
                        act.wait_ge(w_in[kind], g * 16 + 32)
                        used = {("q", 0): 0, ("k", 0): 1, ("q", 1): 2, ("k", 1): 3}[(kind, h)]
                        if used >= 2:
                            act.wait_ge(proj_done, ring_step(g, ("A", used)) + 1)
                        else:
                            act.wait_ge(proj_done, ring_step(g, ("A", 2)) - (3 if used == 0 else 1) + 1)
                    split_att(SPLITS[n])

            def slot(g, s, last):
                if s - 1 in V_PAIR and not (last and s - 1 > 2):
                    n = ring_step(g, ("V", s - 1))
                    proj(n, ring_bank(("V", s - 1)), step_dest(("V", s - 1)))
                if not (last and s >= B):
                    softmax_exp(g * B + s)
                if s == 2 and not (isinstance(g, int) and g == 0):
                    weights(g, s, last)
                if not (last and s >= 4):
                    proj(ring_step(g, ("A", s)), ring_bank(("A", s)), step_dest(("A", s)))
                if not (last and s > B):
                    at_part(g * B + s - 1, (s - 1) % B)
                if not (last and s >= B):
                    pt_part(g * B + s)
                if s != 2 or (isinstance(g, int) and g == 0):
                    weights(g, s, last)
                if s == (3 if last else 7):
                    act.wait_ge(check_in, g * 48 + 48)
                    act.activation(check_junk, low_halves, ACT.Copy, accum_out=low_now[:, :])\
                        .then_inc(low_halves_summed, 1)

            for s in range(2, 10):
                slot(0, s, False)
            with act.Fori(1, NG - 1, 1) as g:
                for s in range(2, 10):
                    slot(g, s, False)
            def ffn_weights(c, what, parity):
                n = {"gate": "q", "up": "k", "down": "o"}[what]
                act.wait_ge(ffn_in[n][parity], ffn_loaded(c, parity))
                split_hi(w[n][0][:, parity], raw[n][:, parity])

            for s in range(2, 9):
                if s == 8:
                    turn_hi(2, 0, False)
                slot(NG - 1, s, True)
                if s == 6:
                    ffn_weights(0, "gate", 0)
                if s == 7:
                    ffn_weights(0, "up", 0)
            turn_hi(3, 1, False)

            def silu(c, parity, half):
                act.wait_ge(gate_done, c * 2 + half + 1)
                if not isinstance(c, int) or c > 0:
                    act.wait_ge(h_ready, c * 2 + (half - 1))
                act.activation(nrm[:, half, :], GATE[half][:, :], ACT.Silu, scale=ag_now[:, parity:parity + 1])\
                    .then_inc(silu_done, 1)

            def hidden_hi(c, parity, half):
                act.wait_ge(h_ready, c * 2 + half + 1)
                act.activation(hid[0][:, parity, half * HALF:(half + 1) * HALF], nrm[:, 2 + half, :], ACT.Copy)\
                    .then_inc(h_hi, 1)

            def chunk(c, parity, last=False):
                act.activation(ag_now[:, parity:parity + 1], ag_sb[:, bass.ds(c, 1)], ACT.Copy)\
                    .then_inc(ag_set, 1)
                act.wait_ge(ag_set, c + 1)
                silu(c, parity, 0)
                if last:
                    act.wait_ge(wd_scaled, 1)
                else:
                    ffn_weights(c + 1, "gate", 1 - parity)
                    ffn_weights(c + 1, "up", 1 - parity)
                ffn_weights(c, "down", parity)
                hidden_hi(c, parity, 0)
                silu(c, parity, 1)
                hidden_hi(c, parity, 1)

            chunk(0, 0)
            with act.Fori(0, (FC - 3) // 2, 1) as j:
                chunk(j * 2 + 1, 1)
                chunk(j * 2 + 2, 0)
            chunk(FC - 2, 1)
            chunk(FC - 1, 0, True)

        @block.vector
        def _(dve):
            def row_stats(b):
                dve.bn_stats(stats[:, b, :], y[:, b, :]).then_inc(stats_set, 1)

            def mean_var(n, half):
                for b in range(half * HB, (half + 1) * HB):
                    dve.wait_ge(stats_set, HB * n + b % HB + 1)
                    ins = dve.bn_aggr(mv[:, b, :], stats[:, b, :])
                ins.then_inc(stats_ready, 1)

            def normalise(n, half, residual):
                dve.wait_ge(scale_ready, n + 1)
                if n > 0:
                    dve.wait_ge(turned, DC * n)
                for b in range(half * HB, (half + 1) * HB):
                    dve.tensor_scalar(nrm[:, b % HB, :], y[:, b, :], mv[:, b, 0:1], small[:, 0, b:b + 1],
                                      ALU.subtract, ALU.mult).then_inc(nrm_ready, 1)
                if residual:
                    for b in range(half * HB, (half + 1) * HB):
                        dve.tensor_scalar(y[:, b, :], y[:, b, :], small[:, 1, b:b + 1], small[:, 2, b:b + 1],
                                          ALU.mult, ALU.add).then_inc(residual_set, 1)

            def turn_lo(n, half, scaled):
                for c in range(DC):
                    dve.wait_ge(turned_hi, DC * n + c + 1)
                    part = (slice(None), c, slice(half * HALF, (half + 1) * HALF))
                    if scaled:
                        dve.scalar_tensor_tensor(xT[1][part], TURN[0 if scaled else 1][c][:, :], lnw_sb[:, c:c + 1],
                                                 xT[0][part], ALU.mult, ALU.subtract).then_inc(turned_lo, 1)
                    else:
                        dve.tensor_tensor(xT[1][part], TURN[0 if scaled else 1][c][:, :], xT[0][part], ALU.subtract)\
                            .then_inc(turned_lo, 1)

            def c_part(half):
                for j in range(2):
                    dve.wait_ge(c_hi, 2 * half + j + 1)
                    part = (slice(None), slice(2 * j, 2 * j + 2), slice(half * HALF, (half + 1) * HALF))
                    dve.tensor_tensor(cT[1][part], cstage[j],
                                      cT[0][part], ALU.subtract).then_inc(c_lo, 1)

            dve.memset(rowsum[:, :], 0.0).then_inc(y_added, O_FREE)
            dve.memset(rinv[:, :], 0.0).then_inc(y2_added, DOWN_FREE)
            c_part(0)
            for half in range(2):
                dve.wait_ge(x_in[half], 16 * HB)
                for b in range(half * HB, (half + 1) * HB):
                    row_stats(b)
                mean_var(half, half)
            normalise(0, 0, True)
            dve.wait_ge(consts_in, 16)
            turn_lo(0, 0, True)
            normalise(1, 1, True)
            c_part(1)
            dve.wait_ge(mask_in, 16)
            dve.tensor_scalar(maskadd[:, :, :], mask_u8[:, :, :], -MASKED, MASKED, ALU.mult, ALU.add)\
                .then_inc(mask_ready, 1)
            dve.tensor_reduce(some[:, :], mask_u8[:, :, :], AX.X, ALU.max).then_inc(mask_set, 1)
            turn_lo(1, 1, True)
            dve.wait_ge(mask_set, 1)

            def scores(n, b):
                dve.wait_ge(scores_done, n + 1)
                dve.wait_ge(bm_ready, n + 1)
                dve.tensor_tensor(sc[:, :, :].rearrange("p h n -> p (h n)"), S_BANK[:, 0:GH * S],
                                  bm[:, b % 4, :, :].rearrange("p h n -> p (h n)"), ALU.add)\
                    .then_inc(masked_ready, 1)
                dve.wait_ge(masked_ready, n + 1)
                dve.tensor_reduce(negmax[:, :], sc[:, :, :], AX.X, ALU.max, negate=True).then_inc(max_ready, 1)

            def probs(n, b):
                dve.wait_ge(exp_done, n + 1)
                dve.reciprocal(rinv[:, :], rowsum[:, :]).then_inc(rinv_ready, 1)
                dve.wait_ge(rinv_ready, n + 1)
                for h in range(GH):
                    ins = dve.tensor_scalar(pr[:, h, :], pr[:, h, :], rinv[:, h:h + 1], some[:, b:b + 1],
                                            ALU.mult, ALU.mult)
                ins.then_inc(prob_ready, 1)

            def at_part(n, b):
                dve.wait_ge(at_hi, n + 1)
                dve.tensor_tensor(at[1][:, b % HB, :], PV_BANK[:, 0:GH * S], at[0][:, b % HB, :], ALU.subtract)\
                    .then_inc(at_lo, 1)

            def add_out(n, b):
                dve.wait_ge(o_done, n + 1)
                dve.tensor_tensor(y[:, b, :], O_BANK[b % 2][:, :], y[:, b, :], ALU.add).then_inc(y_added, 1)

            for s in range(2):
                scores(s, s)
                probs(s, s)
                if s == 1:
                    at_part(0, 0)

            def slot(g, s, last):
                if not (last and s >= B):
                    scores(g * B + s, s % B)
                if not (last and s >= B):
                    probs(g * B + s, s % B)
                for b in O_OF[s]:
                    add_out(g * B + b, b)
                if not (last and s > B):
                    at_part(g * B + s - 1, (s - 1) % B)

            with dve.Fori(0, NG - 1, 1) as g:
                for s in range(2, 10):
                    slot(g, s, False)
            def stats_of(b):
                dve.wait_ge(y_added, (NG - 1) * B + b + 1 + O_FREE)
                row_stats(b)

            for s in range(2, 10):
                slot(NG - 1, s, True)
                if s == 5:
                    for b in range(HB):
                        stats_of(b)
                    mean_var(2, 0)
                if s == 6:
                    dve.wait_ge(low_halves_summed, NG)
                    normalise(2, 0, False)
                if s == 7:
                    stats_of(4)
                    turn_lo(2, 0, False)
                    stats_of(5)
                if s == 8:
                    stats_of(6)
                    dve.wait_ge(flag_done, 1)
                    dve.tensor_scalar(lo_used[0:1, 0:1], FLAG[0:1, 0:1], 0.0, None, ALU.is_gt)\
                        .then_inc(flag_set, 1)
            stats_of(7)
            mean_var(3, 1)
            normalise(3, 1, False)

            turn_lo(3, 1, False)

            def hidden(c, half):
                dve.wait_ge(up_done, c * 2 + half + 1)
                dve.wait_ge(silu_done, c * 2 + half + 1)
                if isinstance(c, int) and c == 0:
                    dve.wait_ge(turned, DC * 4)
                dve.scalar_tensor_tensor(nrm[:, 2 + half, :], UP[half][:, :], au_sb[:, bass.ds(c, 1)],
                                         nrm[:, half, :], ALU.mult, ALU.mult).then_inc(h_ready, 1)

            def hidden_lo(c, parity, half):
                dve.wait_ge(h_hi, c * 2 + half + 1)
                part = (slice(None), parity, slice(half * HALF, (half + 1) * HALF))
                dve.tensor_tensor(hid[1][part], nrm[:, 2 + half, :], hid[0][part], ALU.subtract).then_inc(h_lo, 1)

            def add_down(c, b):
                dve.wait_ge(down_done, c * B + b + 1)
                if isinstance(c, int) and c == 0:
                    dve.tensor_copy(y2[:, b, :], DOWN[b % 4][:, :]).then_inc(y2_added, 1)
                else:
                    dve.tensor_tensor(y2[:, b, :], DOWN[b % 4][:, :], y2[:, b, :], ALU.add).then_inc(y2_added, 1)

            def chunk(c, parity, first=False):
                for half in range(2):
                    hidden(c, half)
                    if not first:
                        for b in range(half * HB, (half + 1) * HB):
                            add_down(c - 1, b)
                    hidden_lo(c, parity, half)

            chunk(0, 0, True)
            chunk(1, 1)
            with dve.Fori(0, (FC - 3) // 2, 1) as j:
                chunk(j * 2 + 2, 0)
                chunk(j * 2 + 3, 1)
            hidden(FC - 1, 0)
            for b in range(B):
                add_down(FC - 2, b)
                if b == HB - 1:
                    hidden_lo(FC - 1, 0, 0)
            hidden(FC - 1, 1)
            hidden_lo(FC - 1, 0, 1)
            for b in range(B):
                dve.wait_ge(merge_scaled, b + 1)
                dve.tensor_tensor(y[:, b, :], y[:, b, :], y2[:, b, :], ALU.add).then_inc(merged, 1)
                dve.wait_ge(down_done, (FC - 1) * B + b + 1)
                dve.wait_ge(merged, 2 * b + 1)
                dve.tensor_tensor(y[:, b, :], DOWN[b % 4][:, :], y[:, b, :], ALU.add).then_inc(merged, 1)

        @block.tensor
        def _(pe):
            PARTS = [(0, 0), (0, 1), (1, 0)]
            PARTS_BUT = {"stationary": [(0, 0), (0, 1)], "moving": [(0, 0), (1, 0)]}

            def product(dst, terms, parts=PARTS):
                total = len(terms) * len(parts)
                n = 0
                for stationary, moving in terms:
                    for i, j in parts:
                        mm = pe.matmul(dst, stationary(i), moving(j), start=(n == 0), stop=(n == total - 1))
                        n += 1
                return mm

            def turn(n):
                pe.wait_ge(nrm_ready, HB * (n + 1))
                for c in range(DC):
                    if n % 2:
                        pe.wait_ge(turned_lo, DC * (n - 1) + c + 1)
                    for i in range(HB):
                        mm = pe.transpose(TURN[n // 2][c][:, i * S:(i + 1) * S], nrm[:, i, c * P:(c + 1) * P],
                                          ident[:, :])
                    mm.then_inc(turned, 1)

            def project(bk, kind, h, half):
                src, wt = (xT if kind == "q" else cT), w[kind]
                return product(bank[bk][:, :], [
                    (lambda i, c=c: wt[i][:, h, c * P:(c + 1) * P],
                     lambda j, c=c: src[j][:, c, half * HALF:(half + 1) * HALF]) for c in range(DC)])

            def project_v(bk, pair):
                wt = [w["v"][i][:, :, :].rearrange("p a b -> p (a b)") for i in range(2)]
                for e in range(2):
                    b = 2 * pair + e
                    mm = product(bank[bk][:, e * GH * DH:(e + 1) * GH * DH], [
                        (lambda i, c=c: cT[i][:, c, b * S:(b + 1) * S],
                         lambda j, c=c: wt[j][:, c * GH * DH:(c + 1) * GH * DH]) for c in range(DC)])
                return mm

            def scores(n, b):
                if not isinstance(n, int) or n > 0:
                    pe.wait_ge(masked_ready, n)
                t = slice(b * S, (b + 1) * S)
                for h in range(GH):
                    mm = pe.matmul(S_BANK[:, h * S:(h + 1) * S], q[:, h, t], k[:, h, t], start=True, stop=True)
                mm.then_inc(scores_done, 1)

            def turn_probs(n):
                pe.wait_ge(prob_ready, n + 1)
                if not isinstance(n, int) or n > 0:
                    pe.wait_ge(pt_ready, n)
                for h in range(GH):
                    mm = pe.transpose(T_BANK[:, h * S:(h + 1) * S], pr[:, h, :], ident[:, :])
                mm.then_inc(pt_done, 1)

            def values(n, b):
                pe.wait_ge(pt_ready, n + 1)
                if not isinstance(n, int) or n > 0:
                    pe.wait_ge(at_lo, n)
                for h in range(GH):
                    mm = pe.matmul(PV_BANK[:, h * S:(h + 1) * S], v[:, b, h * DH:(h + 1) * DH], pt[:, h, :],
                                   start=True, stop=True)
                mm.then_inc(pv_done, 1)

            def output(n, b):
                pe.wait_ge(at_lo, n + 1)
                pe.wait_ge(y_added, n + 1)
                product(O_BANK[b % 2][:, :], [
                    (lambda i, h=h: at[i][:, b % HB, h * S:(h + 1) * S],
                     lambda j, h=h: w["o"][j][:, h, :]) for h in range(GH)]).then_inc(o_done, 1)

            pe.wait_ge(pool_init, 4)
            pe.wait_ge(c_lo, 2)
            for n in range(4):
                kind, h = PRO[n]
                pe.wait_ge(w_lo, min(n + 1, 3))
                if n >= NB:
                    pe.wait_ge(proj_ready, n - NB + 1)
                (project(n % NB, kind, h, 0) if kind == "k" else project_v(n % NB, h)).then_inc(proj_done, 1)
            turn(0)
            pe.wait_ge(turned_lo, 4)
            pe.wait_ge(w_lo, 5)
            for n in (4, 5):
                pe.wait_ge(proj_ready, n - NB + 1)
                project(n % NB, "q", PRO[n][1], 0).then_inc(proj_done, 1)
            pe.wait_ge(proj_ready, 6)
            turn(1)
            scores(0, 0)
            pe.wait_ge(turned_lo, 8)
            pe.wait_ge(c_lo, 4)

            def proj_step(g, key):
                what, s = key
                n = ring_step(g, key)
                pe.wait_ge(proj_ready, n - (NB - 1))
                if what == "A":
                    mm = project(ring_bank(key), *a_kind(s))
                else:
                    mm = project_v(ring_bank(key), V_PAIR[s])
                mm.then_inc(proj_done, 1)

            for s in range(2):
                n = 6 if s == 0 else 8
                pe.wait_ge(proj_ready, n - (NB - 1))
                project(n % NB, *a_kind(s)).then_inc(proj_done, 1)
                if s == 1:
                    values(0, 0)
                turn_probs(s)
                if s == 0:
                    project_v(7 % NB, V_PAIR[8]).then_inc(proj_done, 1)
                scores(s + 1, s + 1)

            def slot(g, s, last):
                if not (last and s >= 4):
                    if 4 <= s < 8:
                        n = SPLITS.index(a_kind(s)[0:2])
                        pe.wait_ge(w_lo, split_count(g, n))
                    proj_step(g, ("A", s))
                for b in O_OF[s]:
                    if b == 0:
                        pe.wait_ge(w_lo, split_count(g, 0))
                    output(g * B + b, b)
                if not (last and s > B):
                    values(g * B + s - 1, (s - 1) % B)
                if not (last and s >= B):
                    turn_probs(g * B + s)
                if s in V_PAIR and not (last and s > 2):
                    if s == 5:
                        pe.wait_ge(w_lo, split_count(g, 2))
                    proj_step(g, ("V", s))
                if not (last and s >= B - 1):
                    if s in (3, 7):
                        pe.wait_ge(proj_ready, ring_step(g, ("A", s)) + 1)
                    scores(g * B + s + 1, (s + 1) % B)

            with pe.Fori(0, NG - 1, 1) as g:
                for s in range(2, 10):
                    slot(g, s, False)
            for s in range(2, 10):
                slot(NG - 1, s, True)
                if s == 7:
                    turn(2)
                if s == 8:
                    pe.wait_ge(low_added, NG + 1)
                    pe.matmul(FLAG[0:1, 0:1], low_sum[:, :], ones[:, :], start=True, stop=True).then_inc(flag_done, 1)

            def gate_up(c, parity, half, short):
                cols = slice(half * HALF, (half + 1) * HALF)
                for n, dst, done in (("q", GATE, gate_done), ("k", UP, up_done)):
                    if not isinstance(c, int) or c > 0:
                        pe.wait_ge(h_ready, c * 2 + (half - 1))
                    if half == 0:
                        pe.wait_ge(w_lo, ffn_split(c, "gate" if n == "q" else "up"))
                    product(dst[half][:, :], [
                        (lambda i, c_=c_: w[n][i][:, parity, c_ * P:(c_ + 1) * P],
                         lambda j, c_=c_: xT[j][:, c_, cols]) for c_ in range(DC)],
                        PARTS_BUT["stationary"] if short else PARTS).then_inc(done, 1)

            def down(c, parity, b, short=False):
                if b % HB == 0:
                    pe.wait_ge(h_lo, c * 2 + b // HB + 1)
                pe.wait_ge(y2_added, c * B + (b - 4 + 1 + DOWN_FREE))
                product(DOWN[b % 4][:, :], [
                    (lambda i: hid[i][:, parity, b * S:(b + 1) * S],
                     lambda j: w["o"][j][:, parity, :])],
                    PARTS_BUT["moving"] if short else PARTS).then_inc(down_done, 1)

            def chunk(c, parity, short):
                for half in range(2):
                    gate_up(c, parity, half, short)
                    if half == 0:
                        pe.wait_ge(w_lo, ffn_split(c - 1, "down"))
                    for b in range(half * HB, (half + 1) * HB):
                        down(c - 1, 1 - parity, b, short)

            def ffn(short):
                pe.wait_ge(turned_lo, DC * 3)
                gate_up(0, 0, 0, short)
                turn(3)
                pe.wait_ge(turned_lo, DC * 4)
                gate_up(0, 0, 1, short)
                with pe.Fori(0, (FC - 3) // 2, 1) as j:
                    chunk(j * 2 + 1, 1, short)
                    chunk(j * 2 + 2, 0, short)
                chunk(FC - 2, 1, short)
                gate_up(FC - 1, 0, 0, short)
                pe.wait_ge(w_lo, ffn_split(FC - 2, "down"))
                for b in range(B):
                    down(FC - 2, 1, b, short)
                gate_up(FC - 1, 0, 1, short)

            pe.wait_ge(flag_set, 1)
            pe.sem_inc(flag_seen, 1)
            used = pe.value_load(lo_used[0:1, 0:1], min_val=0, max_val=1)
            with pe.If(used != 0):
                ffn(False)
            with pe.Else():
                ffn(True)
            pe.wait_ge(w_lo, LAST_SPLIT)
            for b in range(B):
                pe.wait_ge(h_lo, (FC - 1) * 2 + b // HB + 1)
                if b < 4:
                    pe.wait_ge(y2_added, (FC - 2) * B + (b + 4) + 1 + DOWN_FREE)
                else:
                    pe.wait_ge(merged, 2 * (b - 4) + 2)
                product(DOWN[b % 4][:, :], [
                    (lambda i: hid[i][:, 0, b * S:(b + 1) * S],
                     lambda j: w["o"][j][:, 0, :])]).then_inc(down_done, 1)


def kernel(**inputs):
    import numpy as np
    import concourse.bacc as bacc
    from concourse.bass_utils import run_bass_kernel_spmd as run

    def a(name):
        return np.asarray(inputs[name])

    def pad(m, axis):
        shape = list(m.shape)
        shape[axis] = FC * P - FF
        return np.concatenate([m, np.zeros(shape, m.dtype)], axis=axis)

    def by_head(m):
        return m.reshape(NG, GH, DH, DC, P).transpose(0, 4, 1, 3, 2).reshape(NG, P, GH * D)

    layouts = {
        "x": a("x"),
        "ctxt": a("ctx_4096").reshape(T, DC, P).transpose(2, 1, 0),
        "mask": a("mask_BxSxS2_bk0").transpose(1, 0, 2),
        "bias": a("L0_xattn_position_bias").reshape(NG, GH, S, S).transpose(0, 2, 1, 3).reshape(NG, S, GH * S),
        "lnw": a("L0_xattn_ln_weight").reshape(DC, P).T,
        "wq": by_head(a("L0_xattn_w_q")),
        "wk": by_head(a("L0_xattn_w_k")),
        "wv": a("L0_xattn_w_v").reshape(NG, GH * DH, DC, P).transpose(0, 3, 2, 1).reshape(NG, P, GH * D),
        "wo": a("L0_xattn_w_out").reshape(D, NG, GH, DH).transpose(1, 3, 2, 0).reshape(NG, P, GH * D),
        "wg": pad(a("L0_ffn_Wg"), 0).reshape(FC, P, DC, P).transpose(0, 3, 2, 1).reshape(FC, P, D),
        "wu": pad(a("L0_ffn_Wu"), 0).reshape(FC, P, DC, P).transpose(0, 3, 2, 1).reshape(FC, P, D),
        "wd": pad(a("L0_ffn_Wd"), 1).reshape(D, FC, P).transpose(1, 2, 0),
        "ag": pad(a("L0_ffn_ag"), 0).reshape(FC, P).T,
        "au": pad(a("L0_ffn_au"), 0).reshape(FC, P).T,
        "ad": a("L0_ffn_ad"),
    }
    nc = bacc.Bacc("TRN2", target_bir_lowering=False, num_devices=1)
    arrays, args = {}, []
    for name, m in layouts.items():
        m = np.ascontiguousarray(m)
        arrays[f"in_{name}"] = m
        args.append(nc.dram_tensor(f"in_{name}", m.shape, mybir.dt.from_np(m.dtype), kind="ExternalInput").ap())
    args.append(nc.dram_tensor("out_0", (B, S, D), mybir.dt.float32, kind="ExternalOutput").ap())
    program(nc, *args)
    return run(nc, [arrays], core_ids=[0]).results[0]["out_0"]
```

```python
import concourse.bass as bass
from concourse import mybir
from contextlib import ExitStack

B, S, D, H, DH = 8, 128, 512, 32, 128
P = 128
T = B * S
DC = D // P
GH = 2
NG = H // GH
HALF = T // 2
HB = B // 2
FF = 1376
FC = -(-FF // P)
EPS = 1e-5
POOL_MERGES = 2
CHECK = FC * P * D // (P * NG)
MASKED = -1e30

PRO = [("k", 0), ("k", 1), ("v", 0), ("v", 1), ("q", 0), ("q", 1), ("A", 0), ("V", 0), ("A", 1)]
RING = [("A", 2), ("V", 2), ("A", 3), ("A", 4), ("A", 5), ("V", 5), ("A", 6), ("V", 6), ("A", 7),
        ("A", 8), ("V", 8), ("A", 9)]
NB = 3
V_PAIR = {2: 3, 5: 0, 6: 1, 8: 2}
O_OF = {2: [], 3: [0], 4: [1, 2], 5: [3], 6: [4], 7: [5], 8: [6], 9: [7]}
SPLIT_PRO = [("k", 0), ("k", 1), ("q", 0), ("q", 1)]
SPLITS = [("o", 0), ("q", 0), ("v", 0), ("k", 0), ("q", 1), ("k", 1)]
SPLIT_OF = {2: [0, 1], 3: [2, 3], 4: [4], 5: [5]}


def ring_step(g, key):
    return g * len(RING) + (len(PRO) + RING.index(key))


LAST_RING = [("A", 2), ("A", 3), ("V", 2)]


def step_number(g, key, last):
    return g * len(RING) + (len(PRO) + (LAST_RING if last else RING).index(key))


def ring_bank(key):
    return RING.index(key) % NB


def a_kind(s):
    return "qkqk"[s % 4], (s % 4) // 2, 1 if s % 8 < 4 else 0


def unit(c, half):
    if isinstance(c, int) and c < 2:
        return 2 * half + c
    return c * 2 + half


def unit_slot(c, half):
    return c if isinstance(c, int) and c < 2 else half


NORM_PARTS = [range(0, HB), range(HB, B), range(0, HB), range(HB, B - 1), range(B - 1, B)]


def split_count(g, n):
    return g * len(SPLITS) + (len(SPLIT_PRO) + n + 1)


def program(nc, x, ctxt, mask, bias, lnw, wq, wk, wv, wo, wg, wu, wd, ag, au, ad, out):
    f32 = mybir.dt.float32
    f32r = mybir.dt.float32r
    u8 = mybir.dt.uint8
    ALU = mybir.AluOpType
    ACT = mybir.ActivationFunctionType
    AX = mybir.AxisListType

    ctx = ExitStack()
    with ctx:
        def sb(name, shape, dt=f32):
            return ctx.enter_context(nc.sbuf_tensor(name, shape, dt))

        inner = ExitStack()

        def phase(name, shape, dt=f32):
            return inner.enter_context(nc.sbuf_tensor(name, shape, dt))

        def sem(name):
            return ctx.enter_context(nc.semaphore(name))

        xT = [sb("xT_hi", [P, DC, T], f32r), sb("xT_lo", [P, DC, T], f32r)]
        cT = [sb("cT_hi", [P, DC, T], f32r), sb("cT_lo", [P, DC, T], f32r)]
        y = sb("y", [P, B, D])
        at = [sb("at_hi", [P, HB, GH * S], f32r), sb("at_lo", [P, HB, GH * S], f32r)]
        raw = {n: sb(f"w{n}_raw", [P, GH, D]) for n in "qkvo"}
        w = {n: [sb(f"w{n}_hi", [P, GH, D], f32r), sb(f"w{n}_lo", [P, GH, D], f32r)] for n in "qkvo"}
        bias_sb = sb("bias_sb", [P, GH, S])
        maskadd = sb("maskadd", [P, B, S])
        ad_sb = maskadd[:, 0:D // S, :].rearrange("p b n -> p (b n)")
        some = sb("some", [P, B])
        bm = sb("bm", [P, 4, GH, S])
        sc = sb("sc", [P, GH, S])
        pr = sb("pr", [P, GH, S])
        pt = sb("pt", [P, GH, S])
        negmax = sb("negmax", [P, GH])
        rowsum = sb("rowsum", [P, GH])
        rinv = sb("rinv", [P, GH])
        ident = sb("ident", [P, P])
        nrm = sb("nrm", [P, HB, D])
        cstage = [raw["o"][:, :, :], bm[:, :, :, :].rearrange("p r h n -> p (r h) n")\
                  .rearrange("p (a r) n -> p a (r n)", a=2)]
        nrm_flat = nrm[:, :, :].rearrange("p b n -> p (b n)")
        checked = nrm_flat[:, 0:3 * CHECK]
        low_halves = checked.bitcast(mybir.dt.uint16).rearrange("p (n e) -> p n e", e=2)[:, :, 0]
        check_junk = nrm_flat[:, 3 * CHECK:3 * CHECK + 3 * CHECK // 2].bitcast(mybir.dt.bfloat16)
        stats = sb("stats", [P, B, 6])
        mv = sb("mv", [P, B, 2])
        small = sb("small", [P, 8, B])
        minus_half = sb("minus_half", [P, B])
        lnw_sb = sb("lnw_sb", [P, DC])
        ag_sb = sb("ag_sb", [P, FC])
        au_sb = sb("au_sb", [P, FC])
        low_now = sb("low_now", [P, 1])
        low_sum = sb("low_sum", [P, 1])
        lo_used = sb("lo_used", [1, 1], mybir.dt.int32)
        ones = sb("ones", [P, 1])
        ag_now = sb("ag_now", [P, 2])
        mask_u8 = sb("mask_u8", [P, B, S], u8)
        warm = sb("warm", [P, 1])

        q = phase("q", [P, GH, T])
        k = phase("k", [P, GH, T])
        v = phase("v", [P, B, GH * DH])
        inner.close()
        hid = [phase("hid_hi", [P, 2, T], f32r), phase("hid_lo", [P, 2, T], f32r)]
        y2 = phase("y2", [P, B, D])
        ctx.enter_context(inner)

        bank = [ctx.enter_context(nc.psum_tensor(f"bank{i}", [P, 512], f32)) for i in range(8)]
        S_BANK, T_BANK, PV_BANK, O_BANK = bank[3], bank[4], bank[5], bank[6:8]
        TURN = [bank[4:8], bank[0:4]]
        O_FREE, DOWN_FREE = 2, 4
        GATE, UP, DOWN = [bank[4], bank[6]], [bank[5], bank[7]], bank[0:4]
        FLAG = bank[0]

        x_in = [sem(f"x_in{i}") for i in range(2)]
        c_in = [sem(f"c_in{i}") for i in range(2)]
        consts_in = sem("consts_in")
        mask_in = sem("mask_in")
        w_in = {n: sem(f"w{n}_in") for n in "qkvo"}
        ffn_in = {n: [sem(f"ffn_w{n}_in{i}") for i in range(2)] for n in "qko"}
        bias_in = sem("bias_in")
        pool_init = sem("pool_init")
        mask_set = sem("mask_set")
        mask_ready = sem("mask_ready")
        stats_set = sem("stats_set")
        residual_set = sem("residual_set")
        stats_ready = sem("stats_ready")
        scale_step = sem("scale_step")
        scale_ready = sem("scale_ready")
        residual_ready = sem("residual_ready")
        nrm_ready = sem("nrm_ready")
        turned = sem("turned")
        turned_hi = sem("turned_hi")
        turned_lo = sem("turned_lo")
        c_hi = sem("c_hi")
        c_lo = sem("c_lo")
        w_hi = sem("w_hi")
        w_lo = sem("w_lo")
        first_v_hi = sem("first_v_hi")
        first_v_lo = sem("first_v_lo")
        proj_done = sem("proj_done")
        proj_ready = sem("proj_ready")
        bm_ready = sem("bm_ready")
        scores_done = sem("scores_done")
        masked_ready = sem("masked_ready")
        max_ready = sem("max_ready")
        exp_done = sem("exp_done")
        rinv_ready = sem("rinv_ready")
        prob_ready = sem("prob_ready")
        pt_done = sem("pt_done")
        pt_ready = sem("pt_ready")
        pv_done = sem("pv_done")
        at_hi = sem("at_hi")
        at_lo = sem("at_lo")
        o_done = sem("o_done")
        y_added = sem("y_added")
        wd_scaled = sem("wd_scaled")
        ag_set = sem("ag_set")
        gate_done = sem("gate_done")
        up_done = sem("up_done")
        silu_done = sem("silu_done")
        h_ready = sem("h_ready")
        h_hi = sem("h_hi")
        h_lo = sem("h_lo")
        down_done = sem("down_done")
        check_in = sem("check_in")
        low_halves_summed = sem("low_halves_summed")
        low_added = sem("low_added")
        flag_done = sem("flag_done")
        flag_set = sem("flag_set")
        flag_seen = sem("flag_seen")
        merge_scaled = sem("merge_scaled")
        merged = sem("merged")
        merged_by_pool = sem("merged_by_pool")
        result_ready = sem("result_ready")
        y2_added = sem("y2_added")
        out_sent = sem("out_sent")

        block = ctx.enter_context(nc.Block())

        ATT_SPLITS = split_count(NG - 1, 0)

        def ffn_split(c, what):
            if what == "down":
                return c * 3 + (ATT_SPLITS + 5)
            first = 1 if isinstance(c, int) and c == 0 else 0
            return c * 3 + (ATT_SPLITS + first + (0 if what == "gate" else 1))

        def ffn_loaded(c, parity):
            return c * 8 + (16 - 8 * parity)

        LAST_SPLIT = ffn_split(FC - 2, "down") + 1

        @block.sync
        def _(sp):
            def load(n, source, g):
                src = source[bass.ds(g, 1), :, :].rearrange("o p n -> p (o n)")
                sp.dma_start(raw[n][:, :, :].rearrange("p h n -> p (h n)"), src).then_inc(w_in[n], 16)

            def load_bias(g):
                sp.dma_start(bias_sb[:, :, :].rearrange("p h n -> p (h n)"),
                             bias[bass.ds(g, 1), :, :].rearrange("o p n -> p (o n)")).then_inc(bias_in, 16)

            def load_c(half):
                for j in range(2):
                    sp.dma_start(cstage[j],
                                 ctxt[:, 2 * j:2 * j + 2, half * HALF:(half + 1) * HALF])\
                        .then_inc(c_in[j], 16)

            def load_x(half):
                for b in range(half * HB, (half + 1) * HB):
                    sp.dma_start(y[:, b, :], x[b, :, :]).then_inc(x_in[half], 16)

            load("k", wk, 0)
            load_c(0)
            load_x(0)
            sp.dma_start(mask_u8[:, :, :], mask).then_inc(mask_in, 16)
            load("v", wv, 0)
            sp.dma_start(lnw_sb[:, :], lnw).then_inc(consts_in, 16)
            load("q", wq, 0)
            load_x(1)
            sp.wait_ge(c_lo, 2)
            load_c(1)
            load_bias(0)
            sp.wait_ge(c_lo, 4)
            load("o", wo, 0)
            sp.dma_start(ag_sb[:, :], ag).then_inc(consts_in, 16)
            sp.dma_start(au_sb[:, :], au).then_inc(consts_in, 16)
            sp.wait_ge(w_lo, 2)
            load("k", wk, 1)
            sp.wait_ge(first_v_lo, 1)
            load("v", wv, 1)
            sp.wait_ge(w_lo, len(SPLIT_PRO))
            load("q", wq, 1)

            def load_check(g):
                for i, source in enumerate((wg, wu, wd)):
                    flat = source.rearrange("c p n -> (c p n)").rearrange("(g p n) -> g p n", g=NG, p=P)
                    sp.dma_start(checked[:, i * CHECK:(i + 1) * CHECK],
                                 flat[bass.ds(g, 1), :, :].rearrange("o p n -> p (o n)")).then_inc(check_in, 16)

            sp.wait_ge(turned, 2 * DC)
            load_check(0)

            def attention_loads(g, more):
                sp.wait_ge(w_lo, split_count(g, 0))
                load("o", wo, g + 1)
                if more:
                    sp.wait_ge(w_lo, split_count(g, 2))
                    load("v", wv, g + 2)
                    sp.wait_ge(w_lo, split_count(g, 4))
                    load("q", wq, g + 2)
                    sp.wait_ge(w_lo, split_count(g, 5))
                    load("k", wk, g + 2)
                sp.wait_ge(bm_ready, g * B + B)
                load_bias(g + 1)
                sp.wait_ge(low_added, g + 2)
                load_check(g + 1)

            with sp.Fori(0, NG - 2, 1) as g:
                attention_loads(g, True)
            attention_loads(NG - 2, False)

            def load_ffn(n, source, c, parity):
                src = source[bass.ds(c, 1), :, :].rearrange("o p n -> p (o n)")
                sp.dma_start(raw[n][:, parity, :], src).then_inc(ffn_in[n][parity], 16)

            for c in range(2):
                if c == 0:
                    sp.wait_ge(w_lo, split_count(NG - 2, 5))
                load_ffn("q", wg, c, c)
                load_ffn("k", wu, c, c)
            sp.wait_ge(w_lo, ATT_SPLITS)
            sp.wait_ge(bm_ready, NG * B)
            sp.dma_start(ad_sb, ad.rearrange("(o n) -> o n", o=1).broadcast_to([P, D])).then_inc(consts_in, 16)
            load_ffn("o", wd, 0, 0)
            load_ffn("o", wd, 1, 1)

            def ffn_loads(c, parity):
                sp.wait_ge(w_lo, ffn_split(c + 1, "up"))
                load_ffn("q", wg, c + 3, 1 - parity)
                load_ffn("k", wu, c + 3, 1 - parity)
                sp.wait_ge(w_lo, ffn_split(c, "down"))
                load_ffn("o", wd, c + 2, parity)

            sp.wait_ge(w_lo, ffn_split(0, "up"))
            load_ffn("q", wg, 2, 0)
            load_ffn("k", wu, 2, 0)
            with sp.Fori(0, (FC - 3) // 2, 1) as j:
                ffn_loads(j * 2, 0)
                ffn_loads(j * 2 + 1, 1)
            sp.wait_ge(w_lo, ffn_split(FC - 3, "down"))
            load_ffn("o", wd, FC - 1, 0)
            for b in range(B):
                sp.wait_ge(result_ready, b + 1)
                sp.dma_start(out[b, :, :], y[:, b, :]).then_inc(out_sent, 16)
            sp.wait_ge(out_sent, 16 * B)

        @block.gpsimd
        def _(pool):
            pool.memset(ident[:, :], 0.0).then_inc(pool_init, 1)
            pool.memset(minus_half[:, :], -0.5).then_inc(pool_init, 1)
            pool.memset(ones[:, :], 1.0).then_inc(pool_init, 1)
            pool.memset(low_sum[:, :], 0.0).then_inc(low_added, 1)
            pool.wait_ge(pool_init, 3)
            pool.affine_select(out=ident[:, :], in_=ident[:, :], compare_op=ALU.not_equal, fill=1.0,
                               base=0, pattern=[[-1, P]], channel_multiplier=1).then_inc(pool_init, 1)
            pool.wait_ge(pool_init, 4)
            steps = [0]

            def link(ins):
                steps[0] += 1
                ins.then_inc(scale_step, 1)
                pool.wait_ge(scale_step, steps[0])

            def scales(n, rms):
                h = slice(NORM_PARTS[n].start, NORM_PARTS[n].stop)
                mean, var = mv[:, h, 0], mv[:, h, 1]
                pool.wait_ge(stats_ready, n + 1)
                if not rms:
                    link(pool.tensor_scalar(small[:, 3, h], var, EPS, 1.0, ALU.add, ALU.mult))
                    pool.tensor_tensor(small[:, 0, h], small[:, 3, h], minus_half[:, h], ALU.pow)\
                        .then_inc(scale_ready, 1)
                    return
                link(pool.tensor_scalar(small[:, 5, h], var, 1.0 + EPS, EPS * EPS, ALU.mult, ALU.add))
                pool.tensor_tensor(small[:, 0, h], small[:, 5, h], minus_half[:, h], ALU.pow)\
                    .then_inc(scale_ready, 1)
                link(pool.tensor_scalar(small[:, 3, h], var, EPS, 1.0, ALU.add, ALU.mult))
                link(pool.tensor_tensor(small[:, 4, h], small[:, 3, h], minus_half[:, h], ALU.pow))
                link(pool.tensor_scalar(small[:, 1, h], small[:, 4, h], 1.0, 1.0, ALU.add, ALU.mult))
                link(pool.tensor_tensor(small[:, 7, h], mean, small[:, 4, h], ALU.mult))
                pool.tensor_scalar(small[:, 2, h], small[:, 7, h], -1.0, 0.0, ALU.mult, ALU.add)\
                    .then_inc(residual_ready, 1)

            def split_lo(count, hi, lo, source):
                pool.wait_ge(w_hi, count)
                pool.tensor_tensor(lo, source, hi, ALU.subtract).then_inc(w_lo, 1)

            def split_att(count, key):
                n, h = key
                part = (slice(None), h) if n in "qk" else (slice(None), slice(None))
                split_lo(count, w[n][0][part], w[n][1][part], raw[n][part])

            def add_bias(n, b):
                pool.tensor_tensor(bm[:, b % 4, :, :], bias_sb[:, :, :],
                                   maskadd[:, b:b + 1, :].broadcast_to([P, GH, S]), ALU.add).then_inc(bm_ready, 1)

            for n in range(2):
                split_att(n + 1, SPLIT_PRO[n])
            scales(0, True)
            for n in range(2, 4):
                split_att(n + 1, SPLIT_PRO[n])
            scales(1, True)
            pool.wait_ge(mask_ready, 1)
            pool.wait_ge(bias_in, 16)
            pool.wait_ge(c_lo, 4)
            for b in range(4):
                add_bias(b, b)

            def slot(g, s, last):
                for n in SPLIT_OF.get(s, []):
                    if not last or n == 0:
                        split_att(split_count(g, n), SPLITS[n])
                if s + 2 < B or not last:
                    if s == 6:
                        pool.wait_ge(bias_in, g * 16 + 32)
                    pool.wait_ge(masked_ready, g * B + (s - 2 + 1))
                    add_bias(g * B + s + 2, (s + 2) % B)

            def add_low(g):
                pool.wait_ge(low_halves_summed, g + 1)
                pool.wait_ge(low_added, g + 1)
                pool.tensor_tensor(low_sum[:, :], low_sum[:, :], low_now[:, :], ALU.add).then_inc(low_added, 1)

            with pool.Fori(0, NG - 1, 1) as g:
                for s in range(2, 10):
                    slot(g, s, False)
                    if s == 8:
                        add_low(g)
            for s in range(2, 8):
                slot(NG - 1, s, True)
                if s == 4:
                    add_low(NG - 1)

            def split_ffn(c, what, parity):
                n = {"gate": "q", "up": "k", "down": "o"}[what]
                split_lo(ffn_split(c, what), w[n][0][:, parity], w[n][1][:, parity], raw[n][:, parity])

            split_ffn(0, "gate", 0)
            split_ffn(0, "up", 0)
            scales(2, False)
            split_ffn(1, "gate", 1)
            split_ffn(1, "up", 1)
            scales(3, False)
            scales(4, False)

            def chunk(c, parity):
                split_ffn(c + 1, "gate", 1 - parity)
                split_ffn(c + 1, "up", 1 - parity)
                split_ffn(c, "down", parity)

            split_ffn(0, "down", 0)
            with pool.Fori(0, (FC - 3) // 2, 1) as j:
                chunk(j * 2 + 1, 1)
                chunk(j * 2 + 2, 0)
            chunk(FC - 2, 1)
            pool.wait_ge(consts_in, 64)
            pool.wait_ge(ffn_in["o"][0], ffn_loaded(FC - 1, 0))
            pool.tensor_tensor(raw["o"][:, 0], raw["o"][:, 0], ad_sb, ALU.mult).then_inc(wd_scaled, 1)
            split_lo(LAST_SPLIT, w["o"][0][:, 0], w["o"][1][:, 0], raw["o"][:, 0])
            for b in range(B):
                pool.wait_ge(y2_added, (FC - 2) * B + b + 1 + DOWN_FREE)
                pool.tensor_tensor(y2[:, b, :], y2[:, b, :], ad_sb, ALU.mult).then_inc(merge_scaled, 1)
            for b in range(B - POOL_MERGES, B):
                pool.wait_ge(merge_scaled, b + 1)
                pool.tensor_tensor(y[:, b, :], y[:, b, :], y2[:, b, :], ALU.add).then_inc(merged_by_pool, 1)

        def evacuated(kind, h, half):
            if kind == "v":
                return v[:, 2 * h:2 * h + 2, :].rearrange("p b n -> p (b n)")
            return (q if kind == "q" else k)[:, h, half * HALF:(half + 1) * HALF]

        def step_dest(key):
            what, s = key
            if what == "A":
                return evacuated(*a_kind(s))
            return evacuated("v", V_PAIR.get(s if s >= 2 else s + 8), 0)

        @block.scalar
        def _(act):
            act.wait_ge(pool_init, 4)
            act.activation(warm[:, :], minus_half[:, 0:1], ACT.Exp).then_inc(pool_init, 1)

            def split_hi(hi, source):
                act.activation(hi, source, ACT.Copy).then_inc(w_hi, 1)

            def split_att(key):
                n, h = key
                part = (slice(None), h) if n in "qk" else (slice(None), slice(None))
                split_hi(w[n][0][part], raw[n][part])

            def split_c(half):
                for j in range(2):
                    act.wait_ge(c_in[j], 16 * (half + 1))
                    act.activation(cT[0][:, 2 * j:2 * j + 2, half * HALF:(half + 1) * HALF],
                                   cstage[j], ACT.Copy)\
                        .then_inc(c_hi, 1)

            def turn_hi(n, half, scaled):
                for c in range(DC):
                    act.wait_ge(turned, DC * n + c + 1)
                    dst = xT[0][:, c, half * HALF:(half + 1) * HALF]
                    if scaled:
                        act.activation(dst, TURN[0 if scaled else 1][c][:, :], ACT.Copy, scale=lnw_sb[:, c:c + 1])\
                            .then_inc(turned_hi, 1)
                    else:
                        act.activation(dst, TURN[0 if scaled else 1][c][:, :], ACT.Copy).then_inc(turned_hi, 1)

            def proj(n, b, dst):
                act.wait_ge(proj_done, n + 1)
                act.activation(dst, bank[b][:, :], ACT.Copy).then_inc(proj_ready, 1)

            def first_proj(n):
                proj(n, n % NB, evacuated(PRO[n][0], PRO[n][1], 0))

            act.wait_ge(w_in["k"], 16)
            split_att(("k", 0))
            split_att(("k", 1))
            split_c(0)
            act.wait_ge(w_in["v"], 16)
            act.activation(w["v"][0][:, :, :], raw["v"][:, :, :], ACT.Copy).then_inc(first_v_hi, 1)
            first_proj(0)
            act.wait_ge(w_in["q"], 16)
            split_att(("q", 0))
            split_att(("q", 1))
            first_proj(1)
            first_proj(2)
            act.wait_ge(consts_in, 16)
            turn_hi(0, 0, True)
            split_c(1)
            first_proj(3)
            first_proj(4)
            turn_hi(1, 1, True)
            first_proj(5)

            def softmax_exp(n):
                act.wait_ge(max_ready, n + 1)
                if not isinstance(n, int) or n > 0:
                    act.wait_ge(pt_done, n)
                for h in range(GH):
                    ins = act.activation(pr[:, h, :], sc[:, h, :], ACT.Exp, bias=negmax[:, h:h + 1],
                                         scale=1.0, accum_out=rowsum[:, h:h + 1])
                ins.then_inc(exp_done, 1)

            def at_part(n, b):
                act.wait_ge(pv_done, n + 1)
                act.activation(at[0][:, b % HB, :], PV_BANK[:, 0:GH * S], ACT.Copy).then_inc(at_hi, 1)

            def pt_part(n):
                act.wait_ge(pt_done, n + 1)
                act.activation(pt[:, :, :].rearrange("p h n -> p (h n)"), T_BANK[:, 0:GH * S], ACT.Copy)\
                    .then_inc(pt_ready, 1)

            proj(6, 6 % NB, step_dest(("A", 0)))
            softmax_exp(0)
            proj(7, 7 % NB, step_dest(("V", 0)))
            pt_part(0)
            softmax_exp(1)
            proj(8, 8 % NB, step_dest(("A", 1)))
            at_part(0, 0)
            pt_part(1)

            def weights(g, s, last):
                for n in SPLIT_OF.get(s, []):
                    if last and n > 0:
                        continue
                    kind, h = SPLITS[n]
                    if kind == "o":
                        act.wait_ge(w_in["o"], g * 16 + 16)
                        if not isinstance(g, int) or g > 0:
                            act.wait_ge(o_done, g * B)
                    elif kind == "v":
                        act.wait_ge(w_in["v"], g * 16 + 32)
                        act.wait_ge(proj_done, ring_step(g, ("V", 2)) + 1)
                    else:
                        act.wait_ge(w_in[kind], g * 16 + 32)
                        used = {("q", 0): 0, ("k", 0): 1, ("q", 1): 2, ("k", 1): 3}[(kind, h)]
                        if used >= 2:
                            act.wait_ge(proj_done, ring_step(g, ("A", used)) + 1)
                        else:
                            act.wait_ge(proj_done, ring_step(g, ("A", 2)) - (3 if used == 0 else 1) + 1)
                    split_att(SPLITS[n])

            def slot(g, s, last):
                if s - 1 in V_PAIR and not last:
                    n = ring_step(g, ("V", s - 1))
                    proj(n, ring_bank(("V", s - 1)), step_dest(("V", s - 1)))
                if not (last and s >= B):
                    softmax_exp(g * B + s)
                if s == 2:
                    weights(g, s, last)
                if not (last and s >= 4):
                    proj(step_number(g, ("A", s), last), ring_bank(("A", s)), step_dest(("A", s)))
                if not (last and s > B):
                    at_part(g * B + s - 1, (s - 1) % B)
                if not (last and s >= B):
                    pt_part(g * B + s)
                if s != 2:
                    weights(g, s, last)
                if s == (3 if last else 7):
                    act.wait_ge(check_in, g * 48 + 48)
                    act.activation(check_junk, low_halves, ACT.Copy, accum_out=low_now[:, :])\
                        .then_inc(low_halves_summed, 1)

            for s in range(2, 10):
                slot(0, s, False)
            with act.Fori(1, NG - 1, 1) as g:
                for s in range(2, 10):
                    slot(g, s, False)
            def ffn_weights(c, what, parity):
                n = {"gate": "q", "up": "k", "down": "o"}[what]
                act.wait_ge(ffn_in[n][parity], ffn_loaded(c, parity))
                split_hi(w[n][0][:, parity], raw[n][:, parity])

            for s in range(2, 9):
                slot(NG - 1, s, True)
                if s == 4:
                    ffn_weights(0, "gate", 0)
                if s == 5:
                    ffn_weights(0, "up", 0)
                if s == 6:
                    proj(step_number(NG - 1, ("V", 2), True), ring_bank(("V", 2)), step_dest(("V", 2)))
                    ffn_weights(1, "gate", 1)
            turn_hi(2, 0, False)
            ffn_weights(1, "up", 1)
            act.activation(warm[:, :], minus_half[:, 0:1], ACT.Silu).then_inc(pool_init, 1)
            turn_hi(3, 1, False)

            def set_ag(c, parity):
                act.activation(ag_now[:, parity:parity + 1], ag_sb[:, bass.ds(c, 1)], ACT.Copy)\
                    .then_inc(ag_set, 1)

            def silu(c, parity, half):
                u, at_slot = unit(c, half), unit_slot(c, half)
                act.wait_ge(gate_done, u + 1)
                if not isinstance(c, int) or u > 1:
                    act.wait_ge(h_ready, u - 1)
                act.activation(nrm[:, at_slot, :], GATE[at_slot][:, :], ACT.Silu,
                               scale=ag_now[:, parity:parity + 1]).then_inc(silu_done, 1)

            def hidden_hi(c, parity, half):
                act.wait_ge(h_ready, unit(c, half) + 1)
                act.activation(hid[0][:, parity, half * HALF:(half + 1) * HALF],
                               nrm[:, 2 + unit_slot(c, half), :], ACT.Copy).then_inc(h_hi, 1)

            def chunk(c, parity, last=False):
                set_ag(c, parity)
                act.wait_ge(ag_set, c + 1)
                silu(c, parity, 0)
                if last:
                    act.wait_ge(wd_scaled, 1)
                else:
                    ffn_weights(c + 1, "gate", 1 - parity)
                    ffn_weights(c + 1, "up", 1 - parity)
                ffn_weights(c, "down", parity)
                hidden_hi(c, parity, 0)
                silu(c, parity, 1)
                hidden_hi(c, parity, 1)

            set_ag(0, 0)
            set_ag(1, 1)
            act.wait_ge(ag_set, 2)
            silu(0, 0, 0)
            silu(1, 1, 0)
            hidden_hi(0, 0, 0)
            hidden_hi(1, 1, 0)
            ffn_weights(0, "down", 0)
            silu(0, 0, 1)
            hidden_hi(0, 0, 1)
            act.wait_ge(up_done, unit(0, 1) + 1)
            ffn_weights(2, "gate", 0)
            ffn_weights(2, "up", 0)
            ffn_weights(1, "down", 1)
            silu(1, 1, 1)
            hidden_hi(1, 1, 1)
            with act.Fori(0, (FC - 3) // 2, 1) as j:
                chunk(j * 2 + 2, 0)
                chunk(j * 2 + 3, 1)
            chunk(FC - 1, 0, True)

        @block.vector
        def _(dve):
            def row_stats(b):
                dve.bn_stats(stats[:, b, :], y[:, b, :]).then_inc(stats_set, 1)

            def mean_var(n):
                for b in NORM_PARTS[n]:
                    dve.wait_ge(stats_set, (B if n >= 2 else 0) + b + 1)
                    ins = dve.bn_aggr(mv[:, b, :], stats[:, b, :])
                ins.then_inc(stats_ready, 1)

            def normalise(n):
                dve.wait_ge(scale_ready, n + 1)
                if n > 0:
                    dve.wait_ge(turned, DC * min(n, 3))
                for b in NORM_PARTS[n]:
                    dve.tensor_scalar(nrm[:, b % HB, :], y[:, b, :], mv[:, b, 0:1], small[:, 0, b:b + 1],
                                      ALU.subtract, ALU.mult).then_inc(nrm_ready, 1)

            def residual(half):
                dve.wait_ge(residual_ready, half + 1)
                for b in range(half * HB, (half + 1) * HB):
                    dve.tensor_scalar(y[:, b, :], y[:, b, :], small[:, 1, b:b + 1], small[:, 2, b:b + 1],
                                      ALU.mult, ALU.add).then_inc(residual_set, 1)

            def turn_lo(n, half, scaled):
                for c in range(DC):
                    dve.wait_ge(turned_hi, DC * n + c + 1)
                    part = (slice(None), c, slice(half * HALF, (half + 1) * HALF))
                    if scaled:
                        dve.scalar_tensor_tensor(xT[1][part], TURN[0 if scaled else 1][c][:, :], lnw_sb[:, c:c + 1],
                                                 xT[0][part], ALU.mult, ALU.subtract).then_inc(turned_lo, 1)
                    else:
                        dve.tensor_tensor(xT[1][part], TURN[0 if scaled else 1][c][:, :], xT[0][part], ALU.subtract)\
                            .then_inc(turned_lo, 1)

            def c_part(half):
                for j in range(2):
                    dve.wait_ge(c_hi, 2 * half + j + 1)
                    part = (slice(None), slice(2 * j, 2 * j + 2), slice(half * HALF, (half + 1) * HALF))
                    dve.tensor_tensor(cT[1][part], cstage[j],
                                      cT[0][part], ALU.subtract).then_inc(c_lo, 1)

            dve.memset(rowsum[:, :], 0.0).then_inc(y_added, O_FREE)
            dve.memset(rinv[:, :], 0.0).then_inc(y2_added, DOWN_FREE)
            c_part(0)

            def statistics(half):
                dve.wait_ge(x_in[half], 16 * HB)
                for b in range(half * HB, (half + 1) * HB):
                    row_stats(b)
                mean_var(half)

            statistics(0)
            dve.wait_ge(mask_in, 16)
            dve.tensor_scalar(maskadd[:, :, :], mask_u8[:, :, :], -MASKED, MASKED, ALU.mult, ALU.add)\
                .then_inc(mask_ready, 1)
            dve.tensor_reduce(some[:, :], mask_u8[:, :, :], AX.X, ALU.max).then_inc(mask_set, 1)
            dve.wait_ge(first_v_hi, 1)
            dve.tensor_tensor(w["v"][1][:, :, :], raw["v"][:, :, :], w["v"][0][:, :, :], ALU.subtract)\
                .then_inc(first_v_lo, 1)
            normalise(0)
            statistics(1)
            dve.wait_ge(consts_in, 16)
            turn_lo(0, 0, True)
            normalise(1)
            c_part(1)
            turn_lo(1, 1, True)
            dve.wait_ge(mask_set, 1)

            def scores(n, b):
                dve.wait_ge(scores_done, n + 1)
                dve.wait_ge(bm_ready, n + 1)
                dve.tensor_tensor(sc[:, :, :].rearrange("p h n -> p (h n)"), S_BANK[:, 0:GH * S],
                                  bm[:, b % 4, :, :].rearrange("p h n -> p (h n)"), ALU.add)\
                    .then_inc(masked_ready, 1)
                dve.wait_ge(masked_ready, n + 1)
                dve.tensor_reduce(negmax[:, :], sc[:, :, :], AX.X, ALU.max, negate=True).then_inc(max_ready, 1)

            def probs(n, b):
                dve.wait_ge(exp_done, n + 1)
                dve.reciprocal(rinv[:, :], rowsum[:, :]).then_inc(rinv_ready, 1)
                dve.wait_ge(rinv_ready, n + 1)
                for h in range(GH):
                    ins = dve.tensor_scalar(pr[:, h, :], pr[:, h, :], rinv[:, h:h + 1], some[:, b:b + 1],
                                            ALU.mult, ALU.mult)
                ins.then_inc(prob_ready, 1)

            def at_part(n, b):
                dve.wait_ge(at_hi, n + 1)
                dve.tensor_tensor(at[1][:, b % HB, :], PV_BANK[:, 0:GH * S], at[0][:, b % HB, :], ALU.subtract)\
                    .then_inc(at_lo, 1)

            def add_out(n, b):
                dve.wait_ge(o_done, n + 1)
                dve.tensor_tensor(y[:, b, :], O_BANK[b % 2][:, :], y[:, b, :], ALU.add).then_inc(y_added, 1)

            for s in range(2):
                scores(s, s)
                probs(s, s)
                residual(s)
                if s == 1:
                    at_part(0, 0)

            def slot(g, s, last):
                if not (last and s >= B):
                    scores(g * B + s, s % B)
                if not (last and s >= B):
                    probs(g * B + s, s % B)
                for b in O_OF[s]:
                    add_out(g * B + b, b)
                if not (last and s > B):
                    at_part(g * B + s - 1, (s - 1) % B)

            with dve.Fori(0, NG - 1, 1) as g:
                for s in range(2, 10):
                    slot(g, s, False)
            def stats_of(b):
                dve.wait_ge(y_added, (NG - 1) * B + b + 1 + O_FREE)
                row_stats(b)

            last = (NG - 1) * B
            for s in range(2, B):
                scores(last + s, s)
                if s >= 4:
                    stats_of(s - 4)
                if s == 6:
                    dve.wait_ge(flag_done, 1)
                    dve.tensor_scalar(lo_used[0:1, 0:1], FLAG[0:1, 0:1], 0.0, None, ALU.is_gt)\
                        .then_inc(flag_set, 1)
                if s == 7:
                    mean_var(2)
                probs(last + s, s)
                for b in O_OF[s]:
                    if s < 7:
                        add_out(last + b, b)
                at_part(last + s - 1, s - 1)
            add_out(last + 5, 5)
            dve.wait_ge(low_halves_summed, NG)
            normalise(2)
            at_part(last + 7, 7)
            turn_lo(2, 0, False)
            stats_of(4)
            add_out((NG - 1) * B + 6, 6)
            stats_of(5)
            stats_of(6)
            mean_var(3)
            add_out((NG - 1) * B + 7, 7)
            stats_of(7)
            mean_var(4)
            normalise(3)
            normalise(4)
            turn_lo(3, 1, False)

            def hidden(c, half):
                u, at_slot = unit(c, half), unit_slot(c, half)
                dve.wait_ge(up_done, u + 1)
                dve.wait_ge(silu_done, u + 1)
                if isinstance(c, int) and c < 2:
                    if u == 0:
                        dve.wait_ge(turned, DC * 4)
                    if u > 1:
                        dve.wait_ge(h_lo, u - 1)
                dve.scalar_tensor_tensor(nrm[:, 2 + at_slot, :], UP[at_slot][:, :], au_sb[:, bass.ds(c, 1)],
                                         nrm[:, at_slot, :], ALU.mult, ALU.mult).then_inc(h_ready, 1)

            def hidden_lo(c, parity, half):
                dve.wait_ge(h_hi, unit(c, half) + 1)
                part = (slice(None), parity, slice(half * HALF, (half + 1) * HALF))
                dve.tensor_tensor(hid[1][part], nrm[:, 2 + unit_slot(c, half), :], hid[0][part], ALU.subtract)\
                    .then_inc(h_lo, 1)

            def add_down(c, b):
                dve.wait_ge(down_done, c * B + b + 1)
                if isinstance(c, int) and c == 0:
                    dve.tensor_copy(y2[:, b, :], DOWN[b % 4][:, :]).then_inc(y2_added, 1)
                else:
                    dve.tensor_tensor(y2[:, b, :], DOWN[b % 4][:, :], y2[:, b, :], ALU.add).then_inc(y2_added, 1)

            def half_chunk(c, parity, half):
                hidden(c, half)
                for b in range(half * HB, (half + 1) * HB):
                    add_down(c - 1, b)
                hidden_lo(c, parity, half)

            hidden(0, 0)
            hidden(1, 0)
            hidden_lo(0, 0, 0)
            hidden_lo(1, 1, 0)
            hidden(0, 1)
            hidden_lo(0, 0, 1)
            for b in range(HB):
                add_down(0, b)
            hidden(1, 1)
            hidden_lo(1, 1, 1)
            for b in range(HB, B):
                add_down(0, b)
            with dve.Fori(0, (FC - 3) // 2, 1) as j:
                for c, parity in ((j * 2 + 2, 0), (j * 2 + 3, 1)):
                    for half in range(2):
                        half_chunk(c, parity, half)
            hidden(FC - 1, 0)
            for b in range(B):
                add_down(FC - 2, b)
                if b == HB - 1:
                    hidden_lo(FC - 1, 0, 0)

            def merge(b):
                dve.wait_ge(merge_scaled, b + 1)
                dve.tensor_tensor(y[:, b, :], y[:, b, :], y2[:, b, :], ALU.add).then_inc(merged, 1)

            def finish(b):
                dve.wait_ge(down_done, (FC - 1) * B + b + 1)
                if b < B - POOL_MERGES:
                    dve.wait_ge(merged, b + 1)
                else:
                    dve.wait_ge(merged_by_pool, b - (B - POOL_MERGES) + 1)
                dve.tensor_tensor(y[:, b, :], DOWN[b % 4][:, :], y[:, b, :], ALU.add).then_inc(result_ready, 1)

            merge(0)
            merge(1)
            hidden(FC - 1, 1)
            merge(2)
            hidden_lo(FC - 1, 0, 1)
            for b in range(B):
                if 3 <= b < B - POOL_MERGES:
                    merge(b)
                finish(b)

        @block.tensor
        def _(pe):
            PARTS = [(0, 0), (0, 1), (1, 0)]
            PARTS_BUT = {"stationary": [(0, 0), (0, 1)], "moving": [(0, 0), (1, 0)]}

            def product(dst, terms, parts=PARTS, before=None):
                total = len(terms) * len(parts)
                n = 0
                for term, (stationary, moving) in enumerate(terms):
                    if before:
                        before(term)
                    for i, j in parts:
                        mm = pe.matmul(dst, stationary(i), moving(j), start=(n == 0), stop=(n == total - 1))
                        n += 1
                return mm

            def turn(n):
                pe.wait_ge(nrm_ready, HB * (n + 1))
                for c in range(DC):
                    if n % 2:
                        pe.wait_ge(turned_lo, DC * (n - 1) + c + 1)
                    for i in range(HB):
                        mm = pe.transpose(TURN[n // 2][c][:, i * S:(i + 1) * S], nrm[:, i, c * P:(c + 1) * P],
                                          ident[:, :])
                    mm.then_inc(turned, 1)

            def project(bk, kind, h, half, before=None):
                src, wt = (xT if kind == "q" else cT), w[kind]
                return product(bank[bk][:, :], [
                    (lambda i, c=c: wt[i][:, h, c * P:(c + 1) * P],
                     lambda j, c=c: src[j][:, c, half * HALF:(half + 1) * HALF]) for c in range(DC)],
                    before=before)

            def project_v(bk, pair, which=range(2)):
                wt = [w["v"][i][:, :, :].rearrange("p a b -> p (a b)") for i in range(2)]
                for e in which:
                    b = 2 * pair + e
                    mm = product(bank[bk][:, e * GH * DH:(e + 1) * GH * DH], [
                        (lambda i, c=c: cT[i][:, c, b * S:(b + 1) * S],
                         lambda j, c=c: wt[j][:, c * GH * DH:(c + 1) * GH * DH]) for c in range(DC)])
                return mm

            def scores(n, b):
                if not isinstance(n, int) or n > 0:
                    pe.wait_ge(masked_ready, n)
                t = slice(b * S, (b + 1) * S)
                for h in range(GH):
                    mm = pe.matmul(S_BANK[:, h * S:(h + 1) * S], q[:, h, t], k[:, h, t], start=True, stop=True)
                mm.then_inc(scores_done, 1)

            def turn_probs(n):
                pe.wait_ge(prob_ready, n + 1)
                if not isinstance(n, int) or n > 0:
                    pe.wait_ge(pt_ready, n)
                for h in range(GH):
                    mm = pe.transpose(T_BANK[:, h * S:(h + 1) * S], pr[:, h, :], ident[:, :])
                mm.then_inc(pt_done, 1)

            def values(n, b):
                pe.wait_ge(pt_ready, n + 1)
                if not isinstance(n, int) or n > 0:
                    pe.wait_ge(at_lo, n)
                for h in range(GH):
                    mm = pe.matmul(PV_BANK[:, h * S:(h + 1) * S], v[:, b, h * DH:(h + 1) * DH], pt[:, h, :],
                                   start=True, stop=True)
                mm.then_inc(pv_done, 1)

            def output(n, b):
                pe.wait_ge(at_lo, n + 1)
                pe.wait_ge(y_added, n + 1)
                product(O_BANK[b % 2][:, :], [
                    (lambda i, h=h: at[i][:, b % HB, h * S:(h + 1) * S],
                     lambda j, h=h: w["o"][j][:, h, :]) for h in range(GH)]).then_inc(o_done, 1)

            pe.wait_ge(pool_init, 4)

            def first_step(n, before=None):
                kind, h = PRO[n]
                if n >= NB:
                    pe.wait_ge(proj_ready, n - NB + 1)
                if kind == "v":
                    mm = project_v(n % NB, h)
                else:
                    mm = project(n % NB, kind, h, 0, before)
                mm.then_inc(proj_done, 1)

            def context_in(c):
                if c % 2 == 0:
                    pe.wait_ge(c_lo, c // 2 + 1)

            pe.wait_ge(w_lo, 1)
            first_step(0, context_in)
            pe.wait_ge(w_lo, 2)
            first_step(1)
            pe.wait_ge(first_v_lo, 1)
            first_step(2)
            turn(0)
            first_step(3)
            pe.wait_ge(turned_lo, 4)
            pe.wait_ge(w_lo, 3)
            first_step(4)
            turn(1)
            pe.wait_ge(w_lo, 4)
            first_step(5)

            def proj_step(g, key):
                what, s = key
                n = ring_step(g, key)
                pe.wait_ge(proj_ready, n - (NB - 1))
                if what == "A":
                    mm = project(ring_bank(key), *a_kind(s))
                else:
                    mm = project_v(ring_bank(key), V_PAIR[s])
                mm.then_inc(proj_done, 1)

            pe.wait_ge(turned_lo, 8)
            pe.wait_ge(proj_ready, 6 - (NB - 1))
            project(6 % NB, *a_kind(0)).then_inc(proj_done, 1)
            pe.wait_ge(proj_ready, 6)
            scores(0, 0)
            pe.wait_ge(c_lo, 4)
            project_v(7 % NB, V_PAIR[8]).then_inc(proj_done, 1)
            turn_probs(0)
            scores(1, 1)
            project(8 % NB, *a_kind(1)).then_inc(proj_done, 1)
            values(0, 0)
            turn_probs(1)
            scores(2, 2)

            def v_step(g, s):
                if s == 5:
                    pe.wait_ge(w_lo, split_count(g, 2))
                proj_step(g, ("V", s))

            def slot(g, s, last):
                if not (last and s >= 4):
                    if 4 <= s < 8:
                        n = SPLITS.index(a_kind(s)[0:2])
                        pe.wait_ge(w_lo, split_count(g, n))
                    proj_step(g, ("A", s))
                for b in O_OF[s]:
                    if b == 0:
                        pe.wait_ge(w_lo, split_count(g, 0))
                    output(g * B + b, b)
                if not (last and s > B):
                    values(g * B + s - 1, (s - 1) % B)
                if s == 2 and not last:
                    v_step(g, s)
                if not (last and s >= B):
                    turn_probs(g * B + s)
                if s in V_PAIR and s > 2 and not last:
                    v_step(g, s)
                if not (last and s >= B - 1):
                    if s in (3, 7):
                        pe.wait_ge(proj_ready, step_number(g, ("A", s), last) + 1)
                    scores(g * B + s + 1, (s + 1) % B)

            with pe.Fori(0, NG - 1, 1) as g:
                for s in range(2, 10):
                    slot(g, s, False)
            last = (NG - 1) * B
            for s in range(2, 5):
                slot(NG - 1, s, True)
            project_v(ring_bank(("V", 2)), V_PAIR[2], (0,))
            output(last + 3, 3)
            values(last + 4, 4)
            turn_probs(last + 5)
            pe.wait_ge(low_added, NG + 1)
            pe.wait_ge(proj_ready, step_number(NG - 1, ("A", 2), True) + 1)
            pe.matmul(FLAG[0:1, 0:1], low_sum[:, :], ones[:, :], start=True, stop=True).then_inc(flag_done, 1)
            scores(last + 6, 6)
            project_v(ring_bank(("V", 2)), V_PAIR[2], (1,)).then_inc(proj_done, 1)
            output(last + 4, 4)
            values(last + 5, 5)
            pe.wait_ge(flag_set, 1)
            pe.sem_inc(flag_seen, 1)
            used = pe.value_load(lo_used[0:1, 0:1], min_val=0, max_val=1)
            turn_probs(last + 6)
            scores(last + 7, 7)
            output(last + 5, 5)
            pe.wait_ge(proj_ready, step_number(NG - 1, ("V", 2), True) + 1)
            values(last + 6, 6)

            def end_of_attention():
                turn_probs(last + 7)
                output(last + 6, 6)
                values(last + 7, 7)
                turn(2)
                output(last + 7, 7)

            def gate_up(c, parity, half, short, which=("gate", "up")):
                cols = slice(half * HALF, (half + 1) * HALF)
                for what in which:
                    n, dst, done = {"gate": ("q", GATE, gate_done), "up": ("k", UP, up_done)}[what]
                    u, at_slot = unit(c, half), unit_slot(c, half)
                    if not isinstance(c, int) or u > 1:
                        pe.wait_ge(h_ready, u - 1)
                    elif u == 1:
                        pe.wait_ge(y_added, NG * B + O_FREE)
                    if half == 0:
                        pe.wait_ge(w_lo, ffn_split(c, what))
                    product(dst[at_slot][:, :], [
                        (lambda i, c_=c_: w[n][i][:, parity, c_ * P:(c_ + 1) * P],
                         lambda j, c_=c_: xT[j][:, c_, cols]) for c_ in range(DC)],
                        PARTS_BUT["stationary"] if short else PARTS).then_inc(done, 1)

            def down(c, parity, b, short=False):
                if b % HB == 0:
                    pe.wait_ge(h_lo, unit(c, b // HB) + 1)
                pe.wait_ge(y2_added, c * B + (b - 4 + 1 + DOWN_FREE))
                product(DOWN[b % 4][:, :], [
                    (lambda i: hid[i][:, parity, b * S:(b + 1) * S],
                     lambda j: w["o"][j][:, parity, :])],
                    PARTS_BUT["moving"] if short else PARTS).then_inc(down_done, 1)

            def chunk(c, parity, short):
                for half in range(2):
                    gate_up(c, parity, half, short)
                    if half == 0:
                        pe.wait_ge(w_lo, ffn_split(c - 1, "down"))
                    for b in range(half * HB, (half + 1) * HB):
                        down(c - 1, 1 - parity, b, short)

            def ffn(short):
                end_of_attention()
                pe.wait_ge(turned_lo, DC * 3)
                gate_up(0, 0, 0, short)
                gate_up(1, 1, 0, short, ("gate",))
                turn(3)
                gate_up(1, 1, 0, short, ("up",))
                pe.wait_ge(turned_lo, DC * 4)
                for c in range(2):
                    gate_up(c, c, 1, short)
                    if c == 0:
                        pe.wait_ge(w_lo, ffn_split(0, "down"))
                    for b in range(c * HB, (c + 1) * HB):
                        down(0, 0, b, short)
                with pe.Fori(0, (FC - 3) // 2, 1) as j:
                    chunk(j * 2 + 2, 0, short)
                    chunk(j * 2 + 3, 1, short)
                gate_up(FC - 1, 0, 0, short)
                pe.wait_ge(w_lo, ffn_split(FC - 2, "down"))
                for b in range(B):
                    down(FC - 2, 1, b, short)
                gate_up(FC - 1, 0, 1, short)

            with pe.If(used != 0):
                ffn(False)
            with pe.Else():
                ffn(True)
            pe.wait_ge(w_lo, LAST_SPLIT)
            for b in range(B):
                pe.wait_ge(h_lo, (FC - 1) * 2 + b // HB + 1)
                if b < 4:
                    pe.wait_ge(y2_added, (FC - 2) * B + (b + 4) + 1 + DOWN_FREE)
                else:
                    pe.wait_ge(result_ready, b - 4 + 1)
                product(DOWN[b % 4][:, :], [
                    (lambda i: hid[i][:, 0, b * S:(b + 1) * S],
                     lambda j: w["o"][j][:, 0, :])]).then_inc(down_done, 1)


def kernel(**inputs):
    import numpy as np
    import concourse.bacc as bacc
    from concourse.bass_utils import run_bass_kernel_spmd as run

    def a(name):
        return np.asarray(inputs[name])

    def pad(m, axis):
        shape = list(m.shape)
        shape[axis] = FC * P - FF
        return np.concatenate([m, np.zeros(shape, m.dtype)], axis=axis)

    def by_head(m):
        return m.reshape(NG, GH, DH, DC, P).transpose(0, 4, 1, 3, 2).reshape(NG, P, GH * D)

    layouts = {
        "x": a("x"),
        "ctxt": a("ctx_4096").reshape(T, DC, P).transpose(2, 1, 0),
        "mask": a("mask_BxSxS2_bk0").transpose(1, 0, 2),
        "bias": a("L0_xattn_position_bias").reshape(NG, GH, S, S).transpose(0, 2, 1, 3).reshape(NG, S, GH * S),
        "lnw": a("L0_xattn_ln_weight").reshape(DC, P).T,
        "wq": by_head(a("L0_xattn_w_q")),
        "wk": by_head(a("L0_xattn_w_k")),
        "wv": a("L0_xattn_w_v").reshape(NG, GH * DH, DC, P).transpose(0, 3, 2, 1).reshape(NG, P, GH * D),
        "wo": a("L0_xattn_w_out").reshape(D, NG, GH, DH).transpose(1, 3, 2, 0).reshape(NG, P, GH * D),
        "wg": pad(a("L0_ffn_Wg"), 0).reshape(FC, P, DC, P).transpose(0, 3, 2, 1).reshape(FC, P, D),
        "wu": pad(a("L0_ffn_Wu"), 0).reshape(FC, P, DC, P).transpose(0, 3, 2, 1).reshape(FC, P, D),
        "wd": pad(a("L0_ffn_Wd"), 1).reshape(D, FC, P).transpose(1, 2, 0),
        "ag": pad(a("L0_ffn_ag"), 0).reshape(FC, P).T,
        "au": pad(a("L0_ffn_au"), 0).reshape(FC, P).T,
        "ad": a("L0_ffn_ad"),
    }
    nc = bacc.Bacc("TRN2", target_bir_lowering=False, num_devices=1)
    arrays, args = {}, []
    for name, m in layouts.items():
        m = np.ascontiguousarray(m)
        arrays[f"in_{name}"] = m
        args.append(nc.dram_tensor(f"in_{name}", m.shape, mybir.dt.from_np(m.dtype), kind="ExternalInput").ap())
    args.append(nc.dram_tensor("out_0", (B, S, D), mybir.dt.float32, kind="ExternalOutput").ap())
    program(nc, *args)
    return run(nc, [arrays], core_ids=[0]).results[0]["out_0"]
```
